# Optimizing a Trainium2 kernel written in Bass

```python
import numpy as np
import jax
import jax.numpy as jnp

def _softmax(x, axis=-1):
    return jax.nn.softmax(x, axis=axis)

def _gelu(x):
    return jax.nn.gelu(x, approximate=True)

def _silu(x):
    return jax.nn.silu(x)

def _sigmoid(x):
    return jax.nn.sigmoid(x)

def _layernorm(x, axis=-1, eps=1e-05):
    m = jnp.mean(x, axis=axis, keepdims=True)
    v = jnp.var(x, axis=axis, keepdims=True)
    return (x - m) / jnp.sqrt(v + eps)

def _scatter_add(tgt, idx, src, axis=0):
    return tgt.at[idx].add(src)

def _segment_sum(src, seg, n):
    return jax.ops.segment_sum(src, seg, n)
kernel_name = 'mk_flamingo_gated_d2_seqx_r4_fcd771'

def setup_inputs(seed: int=0):
    np.random.seed(seed)
    _w = jnp.asarray

    def _rec_inputs():
        import jax
        import jax.numpy as jnp
        _rk = jax.random.key(seed)
        x = 0.0003765 + 1 * jax.random.normal(jax.random.fold_in(_rk, 1), (16, 256, 512), jnp.float32)
        _lenS = 256 - jax.random.randint(jax.random.fold_in(_rk, 7), (16,), 0, max(1, 256 // 4) + 1, jnp.int32)
        _lenS2 = 256 - jax.random.randint(jax.random.fold_in(_rk, 8), (16,), 0, max(1, 256 // 4) + 1, jnp.int32)
        _ctx_2048P = jax.random.normal(jax.random.fold_in(_rk, 11), (16, 16, 512), jnp.float32)
        _ctx_2048c = jax.random.dirichlet(jax.random.fold_in(_rk, 511), 0.3 * jnp.ones((16,), jnp.float32), (16, 256))
        _ctx_2048t = jnp.einsum('bsk,bkd->bsd', _ctx_2048c, _ctx_2048P)
        _ctx_2048t = _ctx_2048t * jax.lax.rsqrt(jnp.mean(jnp.square(_ctx_2048t)) + 1e-12) * 0.953939
        ctx_2048 = -0.000292821 + 1.00034 * (_ctx_2048t + 0.3 * jax.random.normal(jax.random.fold_in(_rk, 611), (16, 256, 512), jnp.float32))
        _validS = jnp.arange(256)[None, :] < _lenS[:, None]
        _validS2 = jnp.arange(256)[None, :] < _lenS2[:, None]
        _causal = jnp.tril(jnp.ones((256, 256), dtype=bool))
        mask_Bx1x2048_fk1 = jnp.where(jnp.ones((16, 1, 512), dtype=bool), 1.0, 0.0).astype(jnp.float32)
        _g = jax.random.normal(jax.random.fold_in(_rk, 9001), (2, 2), jnp.float32)
        _g = jnp.sign(_g) * jnp.maximum(jnp.abs(_g), 1.0) + (_g == 0) * 1.0
        g_xattn = _g[0]
        g_ffn = _g[1]
        return (x, ctx_2048, mask_Bx1x2048_fk1, g_xattn, g_ffn)
    x, ctx_2048, mask_Bx1x2048_fk1, g_xattn, g_ffn = _rec_inputs()

    def _L0_xattn_setup():
        import jax, jax.numpy as jnp
        import numpy as np
        key = jax.random.key(seed)
        k1, k2, k3, k4, k5 = jax.random.split(key, 5)
        B, D_MODEL, L = (2, 256, 512)
        HEAD_DIM = 8
        H = D_MODEL // HEAD_DIM
        return {'k': jax.random.normal(k1, (B, D_MODEL, L), dtype=jnp.float32), 'v': jax.random.normal(k2, (B, D_MODEL, L), dtype=jnp.float32), 'q': jax.random.normal(k3, (B, D_MODEL, L), dtype=jnp.float32), 'ssm_kernel': jax.random.normal(k4, (H, L), dtype=jnp.float32), 'D': jax.random.normal(k5, (H,), dtype=jnp.float32), 'head_dim': HEAD_DIM}
    _L0_xattn_all = _L0_xattn_setup()
    _L0_xattn_in = {k: v for k, v in _L0_xattn_all.items() if k in ('ssm_kernel', 'D')}
    del _L0_xattn_all

    def _L0_ffn_setup():
        import jax, jax.numpy as jnp
        import numpy as np
        TOP_K = 2
        NUM_EXPERTS = 8
        key = jax.random.key(seed)
        ks = jax.random.split(key, 8)
        B, T, D, F, FS, E = (2, 256, 512, 192, 384, NUM_EXPERTS)
        s = 0.02
        return {'x': jax.random.normal(ks[0], (B, T, D), dtype=jnp.float32), 'router': jax.random.normal(ks[1], (D, E), dtype=jnp.float32) * s, 'shared_gate': jax.random.normal(ks[2], (D, FS), dtype=jnp.float32) * s, 'shared_up': jax.random.normal(ks[3], (D, FS), dtype=jnp.float32) * s, 'shared_down': jax.random.normal(ks[4], (FS, D), dtype=jnp.float32) * s, 'w_gate': jax.random.normal(ks[5], (E, D, F), dtype=jnp.float32) * s, 'w_up': jax.random.normal(ks[6], (E, D, F), dtype=jnp.float32) * s, 'w_down': jax.random.normal(ks[7], (E, F, D), dtype=jnp.float32) * s}
    _L0_ffn_all = _L0_ffn_setup()
    _L0_ffn_in = {k: v for k, v in _L0_ffn_all.items() if k in ('router', 'shared_gate', 'shared_up', 'shared_down', 'w_gate', 'w_up', 'w_down')}
    del _L0_ffn_all

    def _L1_xattn_setup():
        import math
        import jax, jax.numpy as jnp
        import numpy as np
        SIZE = 256
        HEADS = 16
        HEAD_DIM = SIZE // HEADS
        B, T, S = (2, 512, 512)
        NEG = 1000000.0
        key = jax.random.key(seed)
        ks = jax.random.split(key, 10)
        target = jax.random.normal(ks[0], (B, SIZE, T), dtype=jnp.float32)
        source = jax.random.normal(ks[1], (B, SIZE, S), dtype=jnp.float32)
        target_mask = (jax.random.uniform(ks[2], (B, 1, T)) > 0.1).astype(jnp.float32)
        source_mask = (jax.random.uniform(ks[3], (B, 1, S)) > 0.1).astype(jnp.float32)
        scale = 1.0 / math.sqrt(SIZE)
        Wq = jax.random.normal(ks[4], (SIZE, SIZE), dtype=jnp.float32) * scale
        Wk = jax.random.normal(ks[5], (SIZE, SIZE), dtype=jnp.float32) * scale
        Wv = jax.random.normal(ks[6], (SIZE, SIZE), dtype=jnp.float32) * scale
        bq = jax.random.normal(ks[7], (SIZE,), dtype=jnp.float32) * 0.01
        bk = jax.random.normal(ks[8], (SIZE,), dtype=jnp.float32) * 0.01
        bv = jax.random.normal(ks[9], (SIZE,), dtype=jnp.float32) * 0.01
        return {'target': target, 'source': source, 'target_mask': target_mask, 'source_mask': source_mask, 'Wq': Wq, 'bq': bq, 'Wk': Wk, 'bk': bk, 'Wv': Wv, 'bv': bv}
    _L1_xattn_all = _L1_xattn_setup()
    _L1_xattn_in = {k: v for k, v in _L1_xattn_all.items() if k in ('Wq', 'bq', 'Wk', 'bk', 'Wv', 'bv')}
    del _L1_xattn_all

    def _L1_ffn_setup():
        import jax, jax.numpy as jnp
        import numpy as np
        NUM_EXPERTS = 4
        key = jax.random.key(seed)
        k1, k2, k3 = jax.random.split(key, 3)
        B, N, H = (8, 512, 512)
        E = NUM_EXPERTS
        I = H * 4 // E
        x = jax.random.normal(k1, (B, N, H), dtype=jnp.float32)
        gate_up_proj = jax.random.normal(k2, (E, H, 2 * I), dtype=jnp.float32) * 0.02
        down_proj = jax.random.normal(k3, (E, I, H), dtype=jnp.float32) * 0.02
        return {'x': x, 'gate_up_proj': gate_up_proj, 'down_proj': down_proj}
    _L1_ffn_all = _L1_ffn_setup()
    _L1_ffn_in = {k: v for k, v in _L1_ffn_all.items() if k in ('gate_up_proj', 'down_proj')}
    del _L1_ffn_all
    return {'x': x, 'ctx_2048': ctx_2048, 'mask_Bx1x2048_fk1': mask_Bx1x2048_fk1, 'g_xattn': g_xattn, 'g_ffn': g_ffn, 'L0_xattn_ssm_kernel': _L0_xattn_in['ssm_kernel'], 'L0_xattn_D': _L0_xattn_in['D'], 'L0_ffn_router': _L0_ffn_in['router'], 'L0_ffn_shared_gate': _L0_ffn_in['shared_gate'], 'L0_ffn_shared_up': _L0_ffn_in['shared_up'], 'L0_ffn_shared_down': _L0_ffn_in['shared_down'], 'L0_ffn_w_gate': _L0_ffn_in['w_gate'], 'L0_ffn_w_up': _L0_ffn_in['w_up'], 'L0_ffn_w_down': _L0_ffn_in['w_down'], 'L1_xattn_Wq': _L1_xattn_in['Wq'], 'L1_xattn_bq': _L1_xattn_in['bq'], 'L1_xattn_Wk': _L1_xattn_in['Wk'], 'L1_xattn_bk': _L1_xattn_in['bk'], 'L1_xattn_Wv': _L1_xattn_in['Wv'], 'L1_xattn_bv': _L1_xattn_in['bv'], 'L1_ffn_gate_up_proj': _L1_ffn_in['gate_up_proj'], 'L1_ffn_down_proj': _L1_ffn_in['down_proj']}

def reference(x, ctx_2048, mask_Bx1x2048_fk1, g_xattn, g_ffn, L0_xattn_ssm_kernel, L0_xattn_D, L0_ffn_router, L0_ffn_shared_gate, L0_ffn_shared_up, L0_ffn_shared_down, L0_ffn_w_gate, L0_ffn_w_up, L0_ffn_w_down, L1_xattn_Wq, L1_xattn_bq, L1_xattn_Wk, L1_xattn_bk, L1_xattn_Wv, L1_xattn_bv, L1_ffn_gate_up_proj, L1_ffn_down_proj):
    import jax
    import jax.numpy as jnp

    def _L0_xattn_ref(k, v, q, ssm_kernel, D, head_dim):
        import jax, jax.numpy as jnp
        import numpy as np
        B, HD, L = k.shape
        H = HD // head_dim
        fft_size = 2 * L
        k_ = k.reshape(B, H, head_dim, L)
        v_ = v.reshape(B, H, head_dim, L)
        q_ = q.reshape(B, H, head_dim, L)
        kv = jnp.einsum('bhil,bhjl->bijhl', k_, v_)
        kv_f = jnp.fft.rfft(kv, n=fft_size)
        kernel_f = jnp.fft.rfft(ssm_kernel, n=fft_size)
        y = jnp.fft.irfft(kv_f * kernel_f, n=fft_size)[..., :L]
        out = y + kv * D[None, None, None, :, None]
        out = jnp.einsum('bijhl,bhil->bjhl', out, q_)
        out = jnp.transpose(out, (0, 2, 1, 3)).reshape(B, H * head_dim, L)
        return out.astype(k.dtype)

    def _L0_ffn_ref(x, router, shared_gate, shared_up, shared_down, w_gate, w_up, w_down):
        import jax, jax.numpy as jnp
        import numpy as np
        TOP_K = 2
        NUM_EXPERTS = 8
        B, T, D = x.shape
        N = B * T
        E = router.shape[1]
        xf = x.reshape(N, D)
        shared = jax.nn.silu(xf @ shared_gate) * (xf @ shared_up) @ shared_down
        probs = jax.nn.softmax(xf @ router, axis=-1)
        topk_vals, topk_ids = jax.lax.top_k(probs, TOP_K)
        cw = jnp.zeros((N, E), dtype=xf.dtype).at[jnp.arange(N)[:, None], topk_ids].set(topk_vals)
        gated = jax.nn.silu(jnp.einsum('nd,edf->enf', xf, w_gate))
        up = jnp.einsum('nd,edf->enf', xf, w_up)
        y = jnp.einsum('enf,efd->end', gated * up, w_down)
        routed = jnp.einsum('ne,end->nd', cw, y)
        return (shared + routed).reshape(B, T, D)

    def _L1_xattn_ref(target, source, target_mask, source_mask, Wq, bq, Wk, bk, Wv, bv):
        import math
        import jax, jax.numpy as jnp
        import numpy as np
        SIZE = 256
        HEADS = 16
        HEAD_DIM = SIZE // HEADS
        B, T, S = (2, 512, 512)
        NEG = 1000000.0
        b, _, t = target.shape
        s = source.shape[-1]
        q = jnp.einsum('oc,bct->bot', Wq, target) + bq[None, :, None]
        k = jnp.einsum('oc,bcs->bos', Wk, source) + bk[None, :, None]
        v = jnp.einsum('oc,bcs->bos', Wv, source) + bv[None, :, None]
        q = q.reshape(b, HEADS, HEAD_DIM, t)
        k = k.reshape(b, HEADS, HEAD_DIM, s)
        v = v.reshape(b, HEADS, HEAD_DIM, s)
        dot = jnp.einsum('bhdt,bhds->bhts', q, k) / math.sqrt(HEAD_DIM)
        mask = target_mask[:, :, :, None] * source_mask[:, :, None, :]
        dot = mask * dot - (1.0 - mask) * NEG
        amap = jax.nn.softmax(dot, axis=-1) * mask
        out = jnp.einsum('bhts,bhds->bhdt', amap, v)
        return out.reshape(b, HEADS * HEAD_DIM, t)

    def _L1_ffn_ref(x, gate_up_proj, down_proj):
        import jax, jax.numpy as jnp
        import numpy as np
        NUM_EXPERTS = 4
        B, N, H = x.shape
        E, _, two_I = gate_up_proj.shape
        I = two_I // 2
        G = N // E
        x4 = x.reshape(B, G, E, H)
        gu = jnp.einsum('bgeh,ehd->bged', x4, gate_up_proj)
        gate, up = (gu[..., :I], gu[..., I:])
        inter = jax.nn.silu(gate) * up
        out = jnp.einsum('bgei,eih->bgeh', inter, down_proj)
        return out.reshape(B, N, H)
    x = x + jnp.tanh(g_xattn[0]) * _L0_xattn_ref(ctx_2048, ctx_2048, _layernorm(x, axis=-1), L0_xattn_ssm_kernel, L0_xattn_D, 8)
    x = x + jnp.tanh(g_ffn[0]) * _L0_ffn_ref(_layernorm(x, axis=-1), L0_ffn_router, L0_ffn_shared_gate, L0_ffn_shared_up, L0_ffn_shared_down, L0_ffn_w_gate, L0_ffn_w_up, L0_ffn_w_down)
    x = x + jnp.tanh(g_xattn[1]) * _L1_xattn_ref(_layernorm(x, axis=-1), ctx_2048, mask_Bx1x2048_fk1, mask_Bx1x2048_fk1, L1_xattn_Wq, L1_xattn_bq, L1_xattn_Wk, L1_xattn_bk, L1_xattn_Wv, L1_xattn_bv)
    x = x + jnp.tanh(g_ffn[1]) * _L1_ffn_ref(_layernorm(x, axis=-1), L1_ffn_gate_up_proj, L1_ffn_down_proj)
    return x

_drawn_inputs = setup_inputs


def setup_inputs(seed=0):
    import zlib

    import numpy as np

    out = dict(_drawn_inputs(seed))
    spreads = {'g_ffn': (-1.0, 0.6)}
    factors = {'L0_ffn_router': 8.0,
     'L0_ffn_shared_gate': 8.0,
     'L0_ffn_shared_up': 8.0,
     'L0_ffn_shared_down': 8.0,
     'L0_ffn_w_gate': 8.0,
     'L0_ffn_w_up': 8.0,
     'L0_ffn_w_down': 8.0,
     'L1_xattn_Wq': 7.777,
     'L1_xattn_bq': 32.437,
     'L1_xattn_Wk': 7.889,
     'L1_xattn_bk': 200.0,
     'L1_xattn_Wv': 7.553,
     'L1_xattn_bv': 200.0,
     'L1_ffn_gate_up_proj': 8.0,
     'L1_ffn_down_proj': 8.0}
    for name, (base, spread) in spreads.items():
        noise = np.random.default_rng([zlib.crc32(name.encode()), seed]).standard_normal(out[name].shape)
        drawn = base * np.exp(spread * noise) if base else spread * noise
        out[name] = jnp.asarray(drawn.astype(out[name].dtype))
    for name, factor in factors.items():
        out[name] = (out[name] * factor).astype(out[name].dtype)
    return out
```

```python
from contextlib import ExitStack, contextmanager
import concourse.bass as bass
from concourse import mybir
from concourse.alu_op_type import AluOpType as ALU
F32=mybir.dt.float32; F32R=mybir.dt.float32r
ACT=mybir.ActivationFunctionType; AX=mybir.AxisListType

P = 128
B = 16
C = 256
L = 512
EPS = 1e-5


class At:

    def __init__(self, k, u, unroll, count):
        k, u = k + u // unroll, u % unroll
        self.k, self.u, self.unroll, self.count = k, u, unroll, count
        self.n = unroll * k + u

    def back(self, d):
        return At(self.k, self.u - d, self.unroll, self.count)

    @property
    def there(self):
        return not isinstance(self.n, int) or 0 <= self.n < self.count

    def first(self, m):
        return isinstance(self.n, int) and self.n < m

    def of(self, m):
        return self.u % m

    def use(self, m):
        return (self.unroll // m) * self.k + self.u // m


def rolled(eng, step, count, unroll, lag):
    for u in range(unroll):
        step(At(0, u, unroll, count))
    with eng.Fori(1, count // unroll, 1) as k:
        for u in range(unroll):
            step(At(k, u, unroll, count))
    for u in range(lag):
        step(At(count // unroll, u, unroll, count))


def fixed(eng, value, size=1):
    if not isinstance(value, int):
        eng.lower_val(value)
        if size > 1:
            eng.lower_val(value * size)
    return value


@contextmanager
def semaphores(nc, prefix):
    made = []

    def sem(name):
        made.append(nc.alloc_semaphore(name=f"{prefix}_{name}"))
        return made[-1]

    yield sem
    nc.all_engine_barrier()
    nc.clear_and_free_semaphores(made)
    nc.all_engine_barrier()


def mix_phase(nc, x_rows, ctx_t, taps_in, skip_in, g, taps_pad, x1):
    HEADS = 32
    HD = C // HEADS
    LB = L // P
    PAIRW = HD * B
    HALF = 2 * PAIRW + 2 * B
    SLOTW = (HD + 3) * B
    PADW = L + P
    with ExitStack() as ctx:
        sb = lambda n, s, d=F32: ctx.enter_context(nc.sbuf_tensor(n, s, d))
        sem = ctx.enter_context(semaphores(nc, "mix"))
        pad = sb("pad", [HEADS, PADW])
        skip = sb("skip", [HEADS, 1])
        xr = sb("xr", [P, 4, L])
        cT = sb("cT", [P, 2, LB, HD + 3, B])
        skew = sb("skew", [P, 2, L])
        kv = sb("kv", [P, 2, LB, 2, HALF])
        stats = sb("stats", [P, 6])
        mv = sb("mv", [P, 2, 2])
        vare = sb("vare", [P, 1])
        mhalf = sb("mhalf", [P, 1])
        rstd = sb("rstd", [P, 1])
        xn = sb("xn", [P, L])
        qq = sb("qq", [P, 2, LB, 2 * PAIRW])
        z = sb("z", [P, LB, 8, SLOTW])
        o = sb("o", [P, 2, LB, SLOTW])
        y1 = sb("y1", [P, 2, L])
        ident = sb("ident", [P, P])
        gt = sb("gt", [P, 1])
        th = sb("th", [P, 1])
        psY = [ctx.enter_context(nc.psum_tensor(f"psY{i}", [P, 2, 512], F32)) for i in range(2)]
        psQ = ctx.enter_context(nc.psum_tensor("psQ", [P, L], F32))
        psO = ctx.enter_context(nc.psum_tensor("psO", [P, L], F32))

        skip_in_ok = sem("skip_in"); g_in_ok = sem("g_in"); taps_in_ok = sem("taps_in")
        pad_zero = sem("pad_zero"); pad_ok = sem("pad_ok"); pad_out = sem("pad_out")
        ident_zero = sem("ident_zero"); ident_ok = sem("ident_ok"); z_zero = sem("z_zero")
        mhalf_ok = sem("mhalf_ok"); tanh_ok = sem("tanh_ok")
        bn_ok = sem("bn_ok"); mv_ok = sem("mv_ok"); vare_ok = sem("vare_ok")
        rstd_ok = sem("rstd_ok"); xn_ok = sem("xn_ok"); qt_ok = sem("qt_ok")
        qq_ok = sem("qq_ok"); kv_ok = sem("kv_ok"); conv_ok = sem("conv_ok")
        z_ok = sem("z_ok"); sum_ok = sem("sum_ok"); wrap_ok = sem("wrap_ok")
        ot_ok = sem("ot_ok"); y1_ok = sem("y1_ok")
        x_in = [sem(f"x_in{u}") for u in range(4)]
        c_in = [sem(f"c_in{u}") for u in range(2)]
        skew_in = [sem(f"skew_in{u}") for u in range(2)]
        stored = [sem(f"stored{u}") for u in range(2)]
        block = ctx.enter_context(nc.Block())
        roll = lambda eng, step: rolled(eng, step, HEADS, 4, 2)

        @block.sync
        def _(sp):
            sp.wait_ge(pad_zero, 1)
            sp.dma_start(pad[:, P - 1:P - 1 + L], taps_in).then_inc(taps_in_ok, 16)
            sp.dma_start(skip[:], skip_in).then_inc(skip_in_ok, 16)
            sp.dma_start(gt[:], g).then_inc(g_in_ok, 16)
            sp.wait_ge(pad_ok, 1)
            sp.dma_start(taps_pad, pad[:]).then_inc(pad_out, 16)
            sp.wait_ge(pad_out, 16)

            def load(t):
                if not t.there:
                    return
                if not t.first(4):
                    sp.wait_ge(y1_ok, t.n - 3)
                sp.dma_start(xr[:, t.of(4), :], x_rows[bass.ds(t.n * P, P), :]).then_inc(x_in[t.of(4)], 16)
                if not t.first(2):
                    sp.wait_ge(kv_ok, 3 * (t.n - 1))
                src = ctx_t[bass.ds(t.n, 1)].rearrange("o p l w -> (o p) l w")
                dst = cT[:, t.of(2)].rearrange("p l i b -> p l (i b)")
                sp.dma_start(dst[:, :, 0:PAIRW], src).then_inc(c_in[t.of(2)], 16)
                sp.dma_start(dst[:, :, PAIRW:], src[:, :, 0:3 * B]).then_inc(c_in[t.of(2)], 16)
                if not t.first(2):
                    sp.wait_ge(conv_ok, LB * (t.n - 1))
                sp.dma_start(skew[:, t.of(2), :], bass.AP(tensor=taps_pad.tensor, offset=t.n * PADW,
                                                          ap=[[1, P], [1, L]])).then_inc(skew_in[t.of(2)], 16)

            roll(sp, load)

        @block.gpsimd
        def _(pool):
            pool.memset(pad[:], 0.0).then_inc(pad_zero, 1)
            pool.memset(ident[:], 0.0).then_inc(ident_zero, 1)
            pool.memset(mhalf[:], -0.5).then_inc(mhalf_ok, 1)
            pool.wait_ge(ident_zero, 1)
            pool.affine_select(out=ident[:], in_=ident[:], compare_op=ALU.not_equal, fill=1.0, base=0,
                               pattern=[[-1, P]], channel_multiplier=1).then_inc(ident_ok, 1)
            pool.memset(z[:], 0.0).then_inc(z_zero, 1)
            pool.wait_ge(mhalf_ok, 1)

            def step(t):
                if not t.there:
                    return
                u = t.of(2)
                pool.wait_ge(c_in[u], 32 * (t.use(2) + 1))
                if not t.first(2):
                    pool.wait_ge(conv_ok, LB * (t.n - 1))
                c = cT[:, u].rearrange("p l i b -> p l (i b)")
                for h in range(2):
                    one = c[:, :, 0:PAIRW].unsqueeze(2).broadcast_to((P, LB, 2, PAIRW))
                    base = c[:, :, 2 * h * B:2 * h * B + PAIRW]
                    other = bass.AP(tensor=base.tensor, offset=base.offset,
                                    ap=[list(base.ap[0]), [SLOTW, LB], [B, 2], [1, PAIRW]])
                    out = kv[:, u, :, h, 0:2 * PAIRW].rearrange("p l (r w) -> p l r w", r=2)
                    pool.tensor_tensor(out, one, other, ALU.mult).then_inc(kv_ok, 1)
                pool.tensor_tensor(kv[:, u, :, :, 2 * PAIRW:],
                                   c[:, :, 0:4 * B].rearrange("p l (h w) -> p l h w", h=2),
                                   c[:, :, 4 * B:8 * B].rearrange("p l (h w) -> p l h w", h=2),
                                   ALU.mult).then_inc(kv_ok, 1)
                pool.wait_ge(vare_ok, t.n + 1)
                if not t.first(1):
                    pool.wait_ge(xn_ok, t.n)
                pool.tensor_tensor(rstd[:], vare[:], mhalf[:], ALU.pow).then_inc(rstd_ok, 1)

            roll(pool, step)

        @block.scalar
        def _(act):
            act.wait_ge(g_in_ok, 16)
            act.activation(th[:], gt[:], ACT.Tanh).then_inc(tanh_ok, 1)
            act.wait_ge(tanh_ok, 1)

            def step(t):
                if t.there:
                    act.wait_ge(qt_ok, t.n + 1)
                    if not t.first(2):
                        act.wait_ge(z_ok, 4 * LB * (t.n - 1))
                    src = psQ[:].rearrange("p (l w) -> p l w", l=LB)
                    for c in range(2):
                        act.activation(qq[:, t.of(2), :, c * PAIRW:(c + 1) * PAIRW], src, ACT.Copy,
                                       scale=th[:, 0:1]).then_inc(qq_ok, 1)
                t = t.back(2)
                if t.there:
                    act.wait_ge(y1_ok, t.n + 1)
                    act.dma_start(x1[bass.ds(t.n * P, P), :], y1[:, t.of(2), :]).then_inc(stored[t.of(2)], 16)

            roll(act, step)
            for u in range(2):
                act.wait_ge(stored[u], 16 * (HEADS // 2))

        @block.tensor
        def _(pe):
            pe.wait_ge(ident_ok, 1)

            def step(t):
                a, h, w = t, t.back(1), t.back(2)
                for ob in range(LB):
                    if ob == 1 and a.there:
                        pe.wait_ge(xn_ok, a.n + 1)
                        if not a.first(1):
                            pe.wait_ge(qq_ok, 2 * a.n)
                        for l in range(LB):
                            mm = pe.transpose(psQ[:, l * P:(l + 1) * P], xn[:, l * P:(l + 1) * P], ident[:])
                        mm.then_inc(qt_ok, 1)
                    if ob == 2 and w.there:
                        pe.wait_ge(wrap_ok, w.n + 1)
                        if not w.first(1):
                            pe.wait_ge(y1_ok, w.n)
                        for l in range(LB):
                            mm = pe.transpose(psO[:, l * P:(l + 1) * P], o[:, w.of(2), l, 0:PAIRW], ident[:])
                        mm.then_inc(ot_ok, 1)
                    if h.there:
                        u = h.of(2)
                        if ob == 0:
                            pe.wait_ge(kv_ok, 3 * (h.n + 1))
                            pe.wait_ge(skew_in[u], 16 * (h.use(2) + 1))
                        i = (LB * h.u + ob) % 2
                        if not (h.first(1) and ob < 2):
                            pe.wait_ge(z_ok, 4 * (LB * h.n + ob - 1))
                        for m in range(ob + 1):
                            for half in range(2):
                                mm = pe.matmul(psY[i][:, half, 0:HALF], skew[:, u, (ob - m) * P:(ob - m + 1) * P],
                                               kv[:, u, m, half, :], start=(m == 0), stop=(m == ob))
                        mm.then_inc(conv_ok, 1)

            roll(pe, step)

        @block.vector
        def _(dve):
            dve.wait_ge(taps_in_ok, 16)
            dve.wait_ge(skip_in_ok, 16)
            dve.tensor_tensor(pad[:, P - 1:P], pad[:, P - 1:P], skip[:], ALU.add).then_inc(pad_ok, 1)
            dve.wait_ge(z_zero, 1)

            def step(t):
                a, h, w = t, t.back(1), t.back(2)
                if a.there:
                    dve.wait_ge(x_in[a.of(4)], 16 * (a.use(4) + 1))
                    if not a.first(1):
                        dve.wait_ge(mv_ok, a.n)
                    dve.bn_stats(stats[:], xr[:, a.of(4), :]).then_inc(bn_ok, 1)
                    now, before = fixed(dve, a.n + 1), fixed(dve, a.n - 1)
                    dve.wait_ge(pad_ok, 1)
                    dve.wait_ge(bn_ok, now)
                    if not a.first(2):
                        dve.wait_ge(xn_ok, before)
                    dve.bn_aggr(mv[:, a.of(2), :], stats[:]).then_inc(mv_ok, 1)
                    dve.wait_ge(mv_ok, a.n + 1)
                    if not a.first(1):
                        dve.wait_ge(rstd_ok, a.n)
                    dve.tensor_scalar(vare[:], mv[:, a.of(2), 1:2], EPS, None, ALU.add).then_inc(vare_ok, 1)
                for ob in range(LB):
                    if ob == 1 and a.there:
                        dve.wait_ge(rstd_ok, a.n + 1)
                        if not a.first(1):
                            dve.wait_ge(qt_ok, a.n)
                        dve.tensor_scalar(xn[:], xr[:, a.of(4), :], mv[:, a.of(2), 0:1], rstd[:, 0:1],
                                          ALU.subtract, ALU.mult).then_inc(xn_ok, 1)
                    if ob == 3 and w.there:
                        dve.wait_ge(ot_ok, w.n + 1)
                        if not w.first(2):
                            dve.wait_ge(stored[w.of(2)], 16 * w.use(2))
                        dve.tensor_tensor(y1[:, w.of(2), :], psO[:], xr[:, w.of(4), :], ALU.add).then_inc(y1_ok, 1)
                    if h.there:
                        if ob == 0:
                            dve.wait_ge(qq_ok, 2 * (h.n + 1))
                            if not h.first(1):
                                dve.wait_ge(sum_ok, h.n)
                        dve.wait_ge(conv_ok, LB * h.n + ob + 1)
                        y = psY[(LB * h.u + ob) % 2]
                        q = qq[:, h.of(2), ob, :]
                        zz = z[:, ob]

                        def shifted(base, dims):
                            return bass.AP(tensor=base.tensor, offset=base.offset, ap=[list(base.ap[0])] + dims)
                        dve.tensor_tensor(
                            shifted(zz, [[2 * SLOTW, 2], [SLOTW, 2], [1, PAIRW]]),
                            y[:, :, 0:2 * PAIRW].rearrange("p h (r w) -> p h r w", r=2),
                            shifted(q, [[2 * B, 2], [B, 2], [1, PAIRW]]), ALU.mult).then_inc(z_ok, 1)
                        dve.tensor_tensor(
                            shifted(zz[:, 4, :], [[4 * B, 2], [2 * B, 2], [1, 2 * B]]),
                            y[:, :, 2 * PAIRW:HALF].unsqueeze(1).broadcast_to((P, 2, 2, 2 * B)),
                            shifted(q[:, 4 * B:], [[4 * B, 2], [2 * B, 2], [1, 2 * B]]), ALU.mult).then_inc(z_ok, 1)
                        dve.tensor_tensor(zz[:, 5, B:B + PAIRW], y[:, 0, PAIRW:2 * PAIRW], q[:, 0:PAIRW],
                                          ALU.mult).then_inc(z_ok, 1)
                        dve.tensor_tensor(
                            shifted(zz[:, 6, 2 * B:], [[SLOTW + B, 2], [1, PAIRW]]),
                            y[:, 1, 0:2 * PAIRW].rearrange("p (r w) -> p r w", r=2),
                            q[:, 0:PAIRW].unsqueeze(1).broadcast_to((P, 2, PAIRW)), ALU.mult).then_inc(z_ok, 1)
                if h.there:
                    dve.wait_ge(z_ok, 4 * LB * (h.n + 1))
                    if not h.first(2):
                        dve.wait_ge(ot_ok, h.n - 1)
                    dve.tensor_reduce(o[:, h.of(2)], z[:].rearrange("p l s w -> p l w s"), AX.X,
                                      ALU.add).then_inc(sum_ok, 1)
                    dve.wait_ge(sum_ok, h.n + 1)
                    oo = o[:, h.of(2)]
                    dve.tensor_tensor(oo[:, :, 0:3 * B], oo[:, :, 0:3 * B], oo[:, :, PAIRW:], ALU.add).then_inc(wrap_ok, 1)

            roll(dve, step)


def ffn_phase(nc, name, load_rows, store_rows, w_gu, w_dn, units, FC, g, experts=0, router=None, spread=None):
    TOP_K = 2
    GROUPS, T = 4, 8
    KD = L // P
    HALVES = T * P // 512
    TH = T // HALVES
    F = FC * P
    CH = HALVES * FC
    GATE = experts > 0
    SPLITS = 3 if GATE else 2
    with ExitStack() as ctx:
        sb = lambda n, s, d=F32: ctx.enter_context(nc.sbuf_tensor(f"{name}_{n}", s, d))
        sem = ctx.enter_context(semaphores(nc, name))
        ps = lambda n, s: ctx.enter_context(nc.psum_tensor(f"{name}_{n}", s, F32))
        xg = sb("xg", [P, T, L])
        stats = sb("stats", [P, T, 6]); mv = sb("mv", [P, T, 2])
        vare = sb("vare", [P, T]); mhalf = sb("mhalf", [P, T]); rstd = sb("rstd", [P, T])
        xn = sb("xn", [P, 2, L])
        zhi = sb("zhi", [P, KD, T * P], F32R); zlo = sb("zlo", [P, KD, T * P], F32R)
        gu_raw = sb("gu_raw", [P, KD, 2 * F]); dn_raw = sb("dn_raw", [P, FC, L])
        gu_hi = sb("gu_hi", [P, KD, 2 * F], F32R); gu_lo = sb("gu_lo", [P, KD, 2 * F], F32R)
        dn_hi = sb("dn_hi", [P, FC, L], F32R); dn_lo = sb("dn_lo", [P, FC, L], F32R)
        act_g = sb("act_g", [P, 2, 512]); hid = sb("hid", [P, 2, 512])
        h_hi = sb("h_hi", [P, FC, T * P], F32R); h_lo = sb("h_lo", [P, FC, T * P], F32R)
        ident = sb("ident", [P, P]); gt = sb("gt", [P, 1]); th = sb("th", [P, 1])
        psG = [ps(f"psG{i}", [P, 512]) for i in range(2)]
        psU = [ps(f"psU{i}", [P, 512]) for i in range(2)]
        psD = [ps(f"psD{i}", [P, 512]) for i in range(2)]
        psC = ps("psC", [P, 512])
        psT = ps("psT", [P, 512])
        psP = [psT, psC]

        x_in = sem("x_in"); g_in = sem("g_in"); gu_in = sem("gu_in"); dn_in = sem("dn_in")
        ident_zero = sem("ident_zero"); ident_ok = sem("ident_ok"); mhalf_ok = sem("mhalf_ok"); tanh_ok = sem("tanh_ok")
        bn_ok = sem("bn_ok"); mv_ok = sem("mv_ok"); vare_ok = sem("vare_ok"); rstd_ok = sem("rstd_ok")
        xn_ok = sem("xn_ok"); zt_ok = sem("zt_ok"); zhi_ok = sem("zhi_ok"); zlo_ok = sem("zlo_ok")
        guhi_ok = sem("guhi_ok"); gulo_ok = sem("gulo_ok"); dnhi_ok = sem("dnhi_ok"); dnlo_ok = sem("dnlo_ok")
        gate_ok = sem("gate_ok"); up_ok = sem("up_ok"); silu_ok = sem("silu_ok")
        hid_ok = sem("hid_ok"); hhi_ok = sem("hhi_ok"); hlo_ok = sem("hlo_ok")
        down_ok = sem("down_ok"); acc_ok = sem("acc_ok"); stored = sem("stored")
        if GATE:
            hid2 = sb("hid2", [P, 2, 512])
            r_raw = sb("r_raw", [P, KD, P]); r_hi = sb("r_hi", [P, KD, P], F32R); r_lo = sb("r_lo", [P, KD, P], F32R)
            spread_raw = sb("spread_raw", [P, F]); spread_r = sb("spread_r", [P, F], F32R)
            lgT = sb("lgT", [P, 512]); lg = sb("lg", [P, T, experts]); ex = sb("ex", [P, T, experts])
            mx = sb("mx", [P, T]); den = sb("den", [P, T]); rden = sb("rden", [P, T])
            above = sb("above", [P, T, experts, experts]); same = sb("same", [P, T, experts, experts])
            lower = sb("lower", [P, experts, experts]); rank = sb("rank", [P, T, experts]); pick = sb("pick", [P, T, experts])
            cw = sb("cw", [P, T, P]); cwT = sb("cwT", [P, T * P], F32R)
            r_in = sem("r_in"); rz_ok = sem("rz_ok"); rhi_ok = sem("rhi_ok"); rlo_ok = sem("rlo_ok")
            spread_in = sem("spread_in"); spread_ok = sem("spread_ok")
            lgt_ok = sem("lgt_ok"); lgs_ok = sem("lgs_ok"); lgb_ok = sem("lgb_ok"); lg_ok = sem("lg_ok")
            sm_ok = sem("sm_ok"); exp_ok = sem("exp_ok"); rank_ok = sem("rank_ok"); low0_ok = sem("low0_ok"); lower_ok = sem("lower_ok")
            cw0_ok = sem("cw0_ok"); cw_ok = sem("cw_ok"); cwt_ok = sem("cwt_ok"); cwhi_ok = sem("cwhi_ok"); cwlo_ok = sem("cwlo_ok")
            cwb_ok = sem("cwb_ok"); hid2_ok = sem("hid2_ok")
        block = ctx.enter_context(nc.Block())
        src_h, src_ok = (hid2, hid2_ok) if GATE else (hid, hid_ok)

        def units_of(eng, grp, first, later, last):
            first(grp * units)
            if units > 1:
                with eng.Fori(1, units, 1) as un:
                    later(grp * units + un)
            last(grp * units + units - 1)

        @block.sync
        def _(sp):
            sp.dma_start(gt[:], g).then_inc(g_in, 16)
            if GATE:
                sp.wait_ge(rz_ok, 1)
                sp.dma_start(r_raw[:, :, 0:experts], router).then_inc(r_in, 16)

            def weights(n, un):
                sp.wait_ge(gulo_ok, n)
                sp.dma_start(gu_raw[:], w_gu[bass.ds(un, 1)].rearrange("o p k f -> (o p) k f")).then_inc(gu_in, 16)
                sp.wait_ge(dnlo_ok, n)
                sp.dma_start(dn_raw[:], w_dn[bass.ds(un, 1)].rearrange("o p k f -> (o p) k f")).then_inc(dn_in, 16)
                if GATE:
                    sp.wait_ge(spread_ok, n)
                    sp.dma_start(spread_raw[:], spread[bass.ds(un, 1)].rearrange("o p f -> (o p) f")).then_inc(spread_in, 16)

            with sp.Fori(0, GROUPS, 1) as grp:
                sp.wait_ge(stored, 16 * grp)
                sp.dma_start(xg[:], load_rows(grp)).then_inc(x_in, 16)
                if GATE:
                    with sp.Fori(0, units, 1) as un:
                        weights(grp * units + un, un)
                else:
                    weights(grp, grp)
                sp.wait_ge(acc_ok, T * units * (grp + 1))
                sp.dma_start(store_rows(grp), xg[:]).then_inc(stored, 16)
            sp.wait_ge(stored, 16 * GROUPS)

        @block.gpsimd
        def _(pool):
            pool.memset(ident[:], 0.0).then_inc(ident_zero, 1)
            pool.memset(mhalf[:], -0.5).then_inc(mhalf_ok, 1)
            if GATE:
                pool.memset(r_raw[:], 0.0).then_inc(rz_ok, 1)
                pool.memset(cwT[:].bitcast(F32), 0.0).then_inc(cw0_ok, 1)
                pool.memset(cw[:], 1.0).then_inc(cw0_ok, 1)
                pool.memset(lower[:], 1.0).then_inc(low0_ok, 1)
                pool.wait_ge(low0_ok, 1)
                pool.affine_select(out=lower[:], in_=lower[:], compare_op=ALU.is_gt, fill=0.0, base=0,
                                   pattern=[[1, experts], [-1, experts]], channel_multiplier=0).then_inc(lower_ok, 1)
            pool.wait_ge(ident_zero, 1)
            pool.affine_select(out=ident[:], in_=ident[:], compare_op=ALU.not_equal, fill=1.0, base=0,
                               pattern=[[-1, P]], channel_multiplier=1).then_inc(ident_ok, 1)
            pool.wait_ge(mhalf_ok, 1)
            with pool.Fori(0, GROUPS, 1) as grp:
                pool.wait_ge(vare_ok, grp + 1)
                pool.wait_ge(xn_ok, T * grp)
                pool.tensor_tensor(rstd[:], vare[:], mhalf[:], ALU.pow).then_inc(rstd_ok, 1)

        @block.scalar
        def _(act):
            act.wait_ge(g_in, 16)
            act.activation(th[:], gt[:], ACT.Tanh).then_inc(tanh_ok, 1)
            if GATE:
                act.wait_ge(r_in, 16)
                act.activation(r_hi[:], r_raw[:], ACT.Copy).then_inc(rhi_ok, 1)
                act.wait_ge(cw0_ok, 2)

            def prepare(grp):
                for t in range(T):
                    act.wait_ge(zt_ok, T * grp + t + 1)
                    act.wait_ge(up_ok, CH * units * grp)
                    act.activation(zhi[:, :, t * P:(t + 1) * P], psP[t % 2][:].rearrange("p (k w) -> p k w", k=KD),
                                   ACT.Copy).then_inc(zhi_ok, 1)
                if GATE:
                    for h in range(HALVES):
                        act.wait_ge(lgt_ok, HALVES * grp + h + 1)
                        act.wait_ge(lgb_ok, HALVES * grp + h)
                        act.activation(lgT[:], psT[:], ACT.Copy).then_inc(lgs_ok, 1)
                    act.wait_ge(sm_ok, 4 * grp + 2)
                    act.wait_ge(cw_ok, grp)
                    act.activation(ex[:], lg[:], ACT.Exp).then_inc(exp_ok, 1)
                    for h in range(HALVES):
                        act.wait_ge(cwt_ok, HALVES * grp + h + 1)
                        act.wait_ge(cwb_ok, CH * units * grp)
                        act.activation(cwT[0:32, h * 512:(h + 1) * 512], psP[h][0:32, :], ACT.Copy).then_inc(cwhi_ok, 1)

            def split_gu(n):
                act.wait_ge(gu_in, 16 * n + 16)
                act.wait_ge(up_ok, CH * n)
                act.wait_ge(gulo_ok, n)
                act.activation(gu_hi[:], gu_raw[:], ACT.Copy).then_inc(guhi_ok, 1)
                if GATE:
                    act.wait_ge(spread_in, 16 * n + 16)
                    act.activation(spread_r[:], spread_raw[:], ACT.Copy).then_inc(spread_ok, 1)

            def split_dn(n):
                act.wait_ge(dn_in, 16 * n + 16)
                act.wait_ge(down_ok, T * n)
                act.wait_ge(dnlo_ok, n)
                act.activation(dn_hi[:], dn_raw[:], ACT.Copy).then_inc(dnhi_ok, 1)

            def hidden(n):
                for i in range(CH + 1):
                    j = CH * n + i
                    if i < CH:
                        act.wait_ge(gate_ok, j + 1)
                        act.wait_ge(hid_ok, j - 1 if i else j)
                        act.activation(act_g[:, i % 2, :], psG[i % 2][:], ACT.Silu).then_inc(silu_ok, 1)
                    if i > 0:
                        h, c = divmod(i - 1, FC)
                        act.wait_ge(src_ok, j)
                        act.wait_ge(down_ok, T * n)
                        act.activation(h_hi[:, c, h * 512:(h + 1) * 512], src_h[:, (i - 1) % 2, :],
                                       ACT.Copy).then_inc(hhi_ok, 1)

            with act.Fori(0, GROUPS, 1) as grp:
                prepare(grp)
                units_of(act, grp, lambda n: (split_gu(n), split_dn(n), hidden(n)),
                         lambda n: (split_gu(n), split_dn(n), hidden(n)), lambda n: None)

        @block.tensor
        def _(pe):
            pe.wait_ge(ident_ok, 1)

            def prepare(grp):
                for t in range(T):
                    pe.wait_ge(xn_ok, T * grp + t + 1)
                    if t >= 2:
                        pe.wait_ge(zlo_ok, T * grp + t - 1)
                    elif GATE:
                        pe.wait_ge(hid2_ok, CH * units * grp)
                        pe.wait_ge(cwlo_ok, HALVES * grp)
                    else:
                        pe.wait_ge(zlo_ok, T * grp)
                    for k in range(KD):
                        mm = pe.transpose(psP[t % 2][:, k * P:(k + 1) * P], xn[:, t % 2, k * P:(k + 1) * P], ident[:])
                    mm.then_inc(zt_ok, 1)
                if GATE:
                    pe.wait_ge(rlo_ok, 1)
                    pe.wait_ge(zlo_ok, T * grp + T)
                    for h in range(HALVES):
                        cols = slice(h * 512, (h + 1) * 512)
                        if h:
                            pe.wait_ge(lgs_ok, HALVES * grp + h)
                        for k in range(KD):
                            pe.matmul(psT[:], r_hi[:, k, :], zhi[:, k, cols], start=(k == 0), stop=False)
                            pe.matmul(psT[:], r_hi[:, k, :], zlo[:, k, cols], start=False, stop=False)
                            mm = pe.matmul(psT[:], r_lo[:, k, :], zhi[:, k, cols], start=False, stop=(k == KD - 1))
                        mm.then_inc(lgt_ok, 1)
                        pe.wait_ge(lgs_ok, HALVES * grp + h + 1)
                        if h:
                            pe.wait_ge(lg_ok, HALVES * grp + h)
                        for t in range(TH):
                            mm = pe.transpose(psC[:, t * P:(t + 1) * P], lgT[:, t * P:(t + 1) * P], ident[:])
                        mm.then_inc(lgb_ok, 1)
                    pe.wait_ge(cw_ok, grp + 1)
                    for h in range(HALVES):
                        for t in range(TH):
                            mm = pe.transpose(psP[h][:, t * P:(t + 1) * P], cw[:, TH * h + t, :], ident[:])
                        mm.then_inc(cwt_ok, 1)
                    pe.wait_ge(cwlo_ok, HALVES * (grp + 1))
                else:
                    pe.wait_ge(zlo_ok, T * grp + T)

            def product(out, w_hi, w_lo, k, cols, x_hi, x_lo, first, last):
                pe.matmul(out, w_hi(k), x_hi(k), start=first, stop=False)
                pe.matmul(out, w_hi(k), x_lo(k), start=False, stop=False)
                return pe.matmul(out, w_lo(k), x_hi(k), start=False, stop=last)

            def hidden(n):
                pe.wait_ge(guhi_ok, n + 1)
                pe.wait_ge(gulo_ok, n + 1)
                if GATE:
                    pe.wait_ge(spread_ok, n + 1)
                for i in range(CH):
                    j = CH * n + i
                    h, c = divmod(i, FC)
                    cols = slice(h * 512, (h + 1) * 512)
                    for out, off, free, done in ((psG[i % 2], 0, silu_ok, gate_ok), (psU[i % 2], F, hid_ok, up_ok)):
                        w = slice(off + c * P, off + (c + 1) * P)
                        pe.wait_ge(free, j - 1 if i else j)
                        for k in range(KD):
                            mm = product(out[:], lambda k: gu_hi[:, k, w], lambda k: gu_lo[:, k, w], k, cols,
                                         lambda k: zhi[:, k, cols], lambda k: zlo[:, k, cols], k == 0, k == KD - 1)
                        mm.then_inc(done, 1)
                    if GATE:
                        pe.wait_ge(hid2_ok, j)
                        pe.matmul(psC[:], spread_r[:, c * P:(c + 1) * P], cwT[:, cols], start=True,
                                  stop=True).then_inc(cwb_ok, 1)

            def down(n):
                pe.wait_ge(dnhi_ok, n + 1)
                pe.wait_ge(dnlo_ok, n + 1)
                for t in range(T):
                    if t % TH == 0:
                        pe.wait_ge(hlo_ok, CH * n + FC * (t // TH + 1))
                    pe.wait_ge(acc_ok, T * n + (t - 1 if t else 0))
                    rows = slice(t * P, (t + 1) * P)
                    for c in range(FC):
                        mm = product(psD[t % 2][:], lambda c: h_hi[:, c, rows], lambda c: h_lo[:, c, rows], c, None,
                                     lambda c: dn_hi[:, c, :], lambda c: dn_lo[:, c, :], c == 0, c == FC - 1)
                    mm.then_inc(down_ok, 1)

            with pe.Fori(0, GROUPS, 1) as grp:
                prepare(grp)
                units_of(pe, grp, hidden, lambda n: (down(n - 1), hidden(n)), down)

        @block.vector
        def _(dve):
            dve.wait_ge(tanh_ok, 1)
            if GATE:
                dve.wait_ge(lower_ok, 1)
                dve.wait_ge(rhi_ok, 1)
                dve.tensor_tensor(r_lo[:], r_raw[:], r_hi[:], ALU.subtract).then_inc(rlo_ok, 1)

            def prepare(grp):
                dve.wait_ge(x_in, 16 * grp + 16)
                for t in range(T):
                    dve.wait_ge(mv_ok, T * grp)
                    dve.bn_stats(stats[:, t, :], xg[:, t, :]).then_inc(bn_ok, 1)
                for t in range(T):
                    now, before = fixed(dve, T * grp + t + 1), fixed(dve, T * grp)
                    dve.wait_ge(tanh_ok, 1)
                    dve.wait_ge(bn_ok, now)
                    dve.wait_ge(xn_ok, before)
                    dve.bn_aggr(mv[:, t, :], stats[:, t, :]).then_inc(mv_ok, 1)
                dve.wait_ge(mv_ok, T * grp + T)
                dve.wait_ge(rstd_ok, grp)
                dve.tensor_scalar(vare[:], mv[:, :, 1], EPS, None, ALU.add).then_inc(vare_ok, 1)
                dve.wait_ge(rstd_ok, grp + 1)
                for t in range(T + 1):
                    if t < T:
                        dve.wait_ge(zt_ok, T * grp + t - 1 if t else T * grp)
                        dve.tensor_scalar(xn[:, t % 2, :], xg[:, t, :], mv[:, t, 0:1], rstd[:, t:t + 1],
                                          ALU.subtract, ALU.mult).then_inc(xn_ok, 1)
                    if t > 0:
                        rows = slice((t - 1) * P, t * P)
                        dve.wait_ge(zhi_ok, T * grp + t)
                        dve.tensor_tensor(zlo[:, :, rows], psP[(t - 1) % 2][:].rearrange("p (k w) -> p k w", k=KD),
                                          zhi[:, :, rows], ALU.subtract).then_inc(zlo_ok, 1)
                if GATE:
                    route(grp)

            def route(grp):
                for h in range(HALVES):
                    dve.wait_ge(lgb_ok, HALVES * grp + h + 1)
                    dve.wait_ge(exp_ok, grp)
                    dve.tensor_copy(lg[:, TH * h:TH * (h + 1), :],
                                    psC[:].rearrange("p (t w) -> p t w", t=TH)[:, :, 0:experts]).then_inc(lg_ok, 1)
                wide = lambda a: a[:].unsqueeze(2).broadcast_to((P, T, experts))
                dve.wait_ge(lg_ok, HALVES * (grp + 1))
                dve.tensor_reduce(mx[:], lg[:], AX.X, ALU.max).then_inc(sm_ok, 1)
                dve.wait_ge(sm_ok, 4 * grp + 1)
                dve.tensor_tensor(lg[:], lg[:], wide(mx), ALU.subtract).then_inc(sm_ok, 1)
                dve.wait_ge(exp_ok, grp + 1)
                dve.tensor_reduce(den[:], ex[:], AX.X, ALU.add).then_inc(sm_ok, 1)
                dve.wait_ge(sm_ok, 4 * grp + 3)
                dve.reciprocal(rden[:], den[:]).then_inc(sm_ok, 1)
                E = experts
                mine = ex[:].unsqueeze(3).broadcast_to((P, T, E, E))
                theirs = ex[:].unsqueeze(2).broadcast_to((P, T, E, E))
                dve.wait_ge(rank_ok, 6 * grp)
                dve.tensor_tensor(above[:], theirs, mine, ALU.is_gt).then_inc(rank_ok, 1)
                dve.tensor_tensor(same[:], theirs, mine, ALU.is_equal).then_inc(rank_ok, 1)
                dve.wait_ge(rank_ok, 6 * grp + 2)
                dve.tensor_tensor(same[:], same[:], lower[:].unsqueeze(1).broadcast_to((P, T, E, E)),
                                  ALU.mult).then_inc(rank_ok, 1)
                dve.wait_ge(rank_ok, 6 * grp + 3)
                dve.tensor_tensor(above[:], above[:], same[:], ALU.add).then_inc(rank_ok, 1)
                dve.wait_ge(rank_ok, 6 * grp + 4)
                dve.tensor_reduce(rank[:], above[:], AX.X, ALU.add).then_inc(rank_ok, 1)
                dve.wait_ge(rank_ok, 6 * grp + 5)
                dve.wait_ge(cw_ok, grp)
                dve.scalar_tensor_tensor(out=pick[:], in0=rank[:], scalar=float(TOP_K), in1=ex[:],
                                         op0=ALU.is_lt, op1=ALU.mult).then_inc(rank_ok, 1)
                dve.wait_ge(rank_ok, 6 * (grp + 1))
                dve.wait_ge(sm_ok, 4 * (grp + 1))
                dve.wait_ge(cwt_ok, HALVES * grp)
                dve.tensor_tensor(cw[:, :, 0:experts], pick[:], wide(rden), ALU.mult).then_inc(cw_ok, 1)
                for h in range(HALVES):
                    cols = slice(h * 512, (h + 1) * 512)
                    dve.wait_ge(cwhi_ok, HALVES * grp + h + 1)
                    dve.tensor_tensor(cwT[32:64, cols], psP[h][0:32, :], cwT[0:32, cols], ALU.subtract).then_inc(cwlo_ok, 1)

            def split_gu(n):
                dve.wait_ge(guhi_ok, n + 1)
                dve.tensor_tensor(gu_lo[:], gu_raw[:], gu_hi[:], ALU.subtract).then_inc(gulo_ok, 1)

            def split_dn(n):
                dve.wait_ge(dnhi_ok, n + 1)
                dve.tensor_tensor(dn_lo[:], dn_raw[:], dn_hi[:], ALU.subtract).then_inc(dnlo_ok, 1)

            def hidden(n):
                for i in range(CH + 1):
                    j = CH * n + i
                    u = i % 2
                    if i < CH:
                        dve.wait_ge(silu_ok, j + 1)
                        dve.wait_ge(up_ok, j + 1)
                        if GATE:
                            dve.wait_ge(hid2_ok, j - 1 if i else j)
                        else:
                            dve.wait_ge(hhi_ok, j - 1 if i else j)
                            dve.wait_ge(hlo_ok, j - 1 if i else j)
                        dve.tensor_tensor(hid[:, u, :], psU[u][:], act_g[:, u, :], ALU.mult).then_inc(hid_ok, 1)
                        if GATE:
                            dve.wait_ge(hid_ok, j + 1)
                            dve.wait_ge(cwb_ok, j + 1)
                            dve.wait_ge(hhi_ok, j - 1 if i else j)
                            dve.wait_ge(hlo_ok, j - 1 if i else j)
                            dve.tensor_tensor(hid2[:, u, :], psC[:], hid[:, u, :], ALU.mult).then_inc(hid2_ok, 1)
                    if i > 0:
                        h, c = divmod(i - 1, FC)
                        cols = slice(h * 512, (h + 1) * 512)
                        dve.wait_ge(hhi_ok, j)
                        dve.tensor_tensor(h_lo[:, c, cols], src_h[:, (i - 1) % 2, :], h_hi[:, c, cols],
                                          ALU.subtract).then_inc(hlo_ok, 1)

            def add(n):
                for t in range(T):
                    dve.wait_ge(down_ok, T * n + t + 1)
                    dve.wait_ge(acc_ok, T * n)
                    dve.scalar_tensor_tensor(out=xg[:, t, :], in0=psD[t % 2][:], scalar=th[:, 0:1], in1=xg[:, t, :],
                                             op0=ALU.mult, op1=ALU.add).then_inc(acc_ok, 1)

            with dve.Fori(0, GROUPS, 1) as grp:
                prepare(grp)
                units_of(dve, grp, lambda n: (split_gu(n), split_dn(n), hidden(n)),
                         lambda n: (split_gu(n), add(n - 1), split_dn(n), hidden(n)), add)


def at_least(eng, sem, value):
    if not isinstance(value, int) or value > 0:
        eng.wait_ge(sem, value)


def rolled_from(eng, step, count, unroll, peel, lag):
    for t in range(peel * unroll):
        step(At(0, t, unroll, count))
    with eng.Fori(peel, count // unroll, 1) as k:
        for u in range(unroll):
            step(At(k, u, unroll, count))
    for u in range(lag):
        step(At(count // unroll, u, unroll, count))


def attention_phase(nc, x2, ctx_rows, mask, mask_t, w_qkv, b_qk, b_v, g, x3):
    HEADS, HD, GH = 16, 16, 4
    GROUPS = HEADS // GH
    N = B * GROUPS
    KC, TB = C // P, L // P
    NEG = 1.0e6
    HI, LO, HI2, MASK, MAX = 0, HD, 2 * HD, 3 * HD, 3 * HD + 3
    ROWS = 3 * HD + 4
    SPILLS = 12
    PIECES = 6
    with ExitStack() as ctx:
        sb = lambda n, s, d=F32: ctx.enter_context(nc.sbuf_tensor(f"att_{n}", s, d))
        sem = ctx.enter_context(semaphores(nc, "att"))
        ps = lambda n, s: ctx.enter_context(nc.psum_tensor(f"att_{n}", s, F32))
        w_hi = sb("w_hi", [P, 3, KC, C], F32R); w_lo = sb("w_lo", [P, 3, KC, C], F32R)
        bqk = sb("bqk", [P, 4]); bqk4 = sb("bqk4", [P, 4]); bv = sb("bv", [P, C])
        gt = sb("gt", [P, 1]); th = sb("th", [P, 1]); ident = sb("ident", [P, P]); mhalf = sb("mhalf", [P, KC])
        xr = sb("xr", [P, KC, L]); cr = sb("cr", [P, KC, L])
        mbc = sb("mbc", [P, L]); mcol = sb("mcol", [P, TB])
        stats = sb("stats", [P, KC, 6]); mv = sb("mv", [P, KC, 2]); vare = sb("vare", [P, KC]); rstd = sb("rstd", [P, KC])
        xn = sb("xn", [P, KC, L])
        xn_hi = sb("xn_hi", [P, KC, L], F32R); xn_lo = sb("xn_lo", [P, KC, L], F32R)
        cr_hi = sb("cr_hi", [P, KC, L], F32R); cr_lo = sb("cr_lo", [P, KC, L], F32R)
        proj = sb("proj", [P, 4, L]); projm = sb("projm", [P, 2, L])
        p_hi = sb("p_hi", [P, 4, L], F32R); p_lo = sb("p_lo", [P, 4, L], F32R)
        mk = sb("mk", [B, L]); neg = sb("neg", [B, L])
        mg = sb("mg", [P, 2, L])
        qk = sb("qk", [P, 4, 2, GH, L], F32R)
        qs, ks = qk[:, :, 0], qk[:, :, 1]
        vtmp = sb("vtmp", [P, 2, 2, C]); va = sb("va", [P, 2, TB, HEADS, 2 * HD])
        nmax = sb("nmax", [P, 2, TB, GH]); mrow = sb("mrow", [GH, 2, L], F32R)
        pt = sb("pt", [P, 4, 2, L])
        osb = sb("osb", [P, L]); den = sb("den", [P, L]); rec = sb("rec", [P, L])
        lay = nc.dram_tensor("att_lay", (B, 2, ROWS, HEADS, L), F32, kind="Internal").ap()
        xs = sb("xs", [P, 4, L]); yo = sb("yo", [P, 2, L])
        psS = [ps(f"psS{i}", [P, L]) for i in range(2)]
        psB = [ps(f"psB{i}", [P, 2, L]) for i in range(2)]
        psO = ps("psO", [P, L]); psM = ps("psM", [P, L])

        c_in = sem("c_in"); ident_zero = sem("ident_zero"); ident_ok = sem("ident_ok"); mhalf_ok = sem("mhalf_ok")
        zero_ok = sem("zero_ok"); tanh_ok = sem("tanh_ok"); whi_ok = sem("whi_ok"); wlo_ok = sem("wlo_ok"); bq_ok = sem("bq_ok")
        x_in = sem("x_in"); ctx_in = sem("ctx_in"); mask_in = sem("mask_in"); mcol_in = sem("mcol_in")
        bn_ok = sem("bn_ok"); mv_ok = sem("mv_ok"); vare_ok = sem("vare_ok"); rstd_ok = sem("rstd_ok"); xn_ok = sem("xn_ok")
        xhi_ok = sem("xhi_ok"); xlo_ok = sem("xlo_ok"); chi_ok = sem("chi_ok"); clo_ok = sem("clo_ok")
        mrow_ok = sem("mrow_ok"); mrow_out = sem("mrow_out"); lay_ok = sem("lay_ok"); mg_ok = sem("mg_ok")
        piece_ok = sem("piece_ok"); proj_ok = sem("proj_ok"); vtmp_ok = sem("vtmp_ok"); v_ok = sem("v_ok")
        projm_ok = sem("projm_ok"); phi_ok = sem("phi_ok"); plo_ok = sem("plo_ok")
        fill_in = [sem(f"fill_in{i}") for i in range(4)]
        s_ok = sem("s_ok"); max_ok = sem("max_ok"); mt_ok = sem("mt_ok"); mcopy_ok = sem("mcopy_ok")
        max_in = [sem(f"max_in{i}") for i in range(2)]
        b_ok = sem("b_ok"); exp_ok = sem("exp_ok"); av_ok = sem("av_ok")
        osb_ok = sem("osb_ok"); den_ok = sem("den_ok"); mk_in = sem("mk_in")
        rec_ok = sem("rec_ok"); recm_ok = sem("recm_ok"); out_ok = sem("out_ok"); y_ok = sem("y_ok")
        xs_in = [sem(f"xs_in{i}") for i in range(4)]
        stored = [sem(f"stored{i}") for i in range(2)]
        block = ctx.enter_context(nc.Block())
        roll = lambda eng, step: rolled_from(eng, step, N, 2 * GROUPS, 1, 8)
        raw = pt[:, 0:3, :, 0:C]
        element = lambda t: At(t.k, t.u // GROUPS, 2, B)

        @block.sync
        def _(sp):
            sp.dma_start(raw, w_qkv).then_inc(c_in, 16)
            sp.dma_start(bqk[:], b_qk).then_inc(c_in, 16)
            sp.dma_start(bv[:], b_v.broadcast_to((P, C))).then_inc(c_in, 16)
            sp.dma_start(gt[:], g).then_inc(c_in, 16)
            sp.dma_start(mk[:], mask).then_inc(mk_in, 16)
            sp.wait_ge(mrow_ok, 8)
            for o in range(2):
                for r in range(4):
                    sp.dma_start(lay[:, o, MASK + r], qk[0:B, 3, o, r, :].bitcast(F32).unsqueeze(1)
                                 .broadcast_to((B, HEADS, L))).then_inc(mrow_out, 16)
            sp.wait_ge(mrow_out, 16 * 8)
            sp.wait_ge(zero_ok, 4)

            def load(b):
                b4, pos = fixed(sp, 4 * b.n), fixed(sp, b.n * L, 4)
                at_least(sp, xn_ok, b.n)
                sp.dma_start(xr[:], bass.AP(tensor=x2.tensor, offset=pos,
                                            ap=[[B * L, P], [P * B * L, KC], [1, L]])).then_inc(x_in, 16)
                at_least(sp, clo_ok, b.n)
                sp.dma_start(cr[:], ctx_rows[bass.ds(b.n, 1)].rearrange("o (k p) s -> (o p) k s", p=P)).then_inc(ctx_in, 16)
                at_least(sp, mg_ok, b.n)
                at_least(sp, projm_ok, b4)
                at_least(sp, v_ok, b4)
                sp.dma_start(mbc[:], mask[bass.ds(b.n, 1), :].broadcast_to((P, L))).then_inc(mask_in, 16)
                sp.dma_start(mcol[:], mask_t[bass.ds(b.n, 1)].rearrange("o p s -> (o p) s")).then_inc(mcol_in, 16)

            def spill(b):
                at, split = fixed(sp, b.n * 2 * ROWS * HEADS * L, 4), fixed(sp, 4 * (b.n + 1))
                sp.wait_ge(plo_ok, split)
                for o in range(2):
                    for row in (HI, LO, HI2):
                        part = p_lo if row == (HI2 if o else LO) else p_hi
                        for j in range(2):
                            sp.dma_start(bass.AP(tensor=lay.tensor, offset=at + ((o * ROWS + row) * HEADS + j * HEADS // 2) * L,
                                                 ap=[[HEADS * L, HD], [L, HEADS // 2], [1, L]]),
                                         part[:, 2 * o + j, :].bitcast(F32)).then_inc(lay_ok, 16)

            def fill(f):
                b, s, a = element(f), f.of(4), f.u % GROUPS
                pos, before = fixed(sp, b.n * L, 4), fixed(sp, f.n - 3)
                at = fixed(sp, b.n * 2 * ROWS * HEADS * L, 4)
                used, out = fixed(sp, 8 * (f.n - 3)), fixed(sp, 16 * SPILLS * (b.n + 1))
                at_least(sp, b_ok, used)
                sp.wait_ge(lay_ok, out)
                for row, end in ((HI, MASK), (MASK, ROWS)):
                    sp.dma_start(qk[row:end, s].rearrange("p o h s -> p o (h s)").bitcast(F32),
                                 bass.AP(tensor=lay.tensor, offset=at + (row * HEADS + a * GH) * L,
                                         ap=[[HEADS * L, end - row], [ROWS * HEADS * L, 2], [1, GH * L]])).then_inc(fill_in[s], 16)
                at_least(sp, y_ok, before)
                for h in range(GH):
                    sp.dma_start(xs[32 * h:32 * h + HD, s, :],
                                 bass.AP(tensor=x2.tensor, offset=pos + (a * GH + h) * HD * B * L,
                                         ap=[[B * L, HD], [1, L]])).then_inc(xs_in[s], 16)

            def store(w):
                b, a = element(w), w.u % GROUPS
                pos = fixed(sp, b.n * L, 4)
                sp.wait_ge(y_ok, w.n + 1)
                for h in range(GH):
                    sp.dma_start(bass.AP(tensor=x3.tensor, offset=pos + (a * GH + h) * (HD // 4) * B * L,
                                         ap=[[B * L, HD // 4], [C // 4 * B * L, 4], [1, L]]),
                                 yo[32 * h:32 * h + HD, w.of(2), :]).then_inc(stored[w.of(2)], 16)

            def step(t):
                if t.u % GROUPS == 0 and t.there:
                    load(element(t))
                if t.back(4).there:
                    fill(t.back(4))
                if t.u % GROUPS == 3 and t.there:
                    spill(element(t))
                if t.back(8).there:
                    store(t.back(8))

            roll(sp, step)
            for i in range(2):
                sp.wait_ge(stored[i], 16 * GH * (N // 2))

        @block.gpsimd
        def _(pool):
            pool.memset(ident[:], 0.0).then_inc(ident_zero, 1)
            pool.memset(mhalf[:], -0.5).then_inc(mhalf_ok, 1)
            pool.wait_ge(ident_zero, 1)
            pool.affine_select(out=ident[:], in_=ident[:], compare_op=ALU.not_equal, fill=1.0, base=0,
                               pattern=[[-1, P]], channel_multiplier=1).then_inc(ident_ok, 1)
            pool.memset(qk[:, 0:3].bitcast(F32), 0.0).then_inc(zero_ok, 1)
            pool.memset(xs[:], 0.0).then_inc(zero_ok, 1)
            pool.wait_ge(c_in, 64)
            pool.wait_ge(whi_ok, 1)
            pool.tensor_tensor(w_lo[:], raw, w_hi[:], ALU.subtract).then_inc(wlo_ok, 1)
            pool.wait_ge(mhalf_ok, 1)
            pool.wait_ge(mrow_out, 16 * 8)
            pool.memset(qk[:, 3].bitcast(F32), 0.0).then_inc(zero_ok, 1)

            def finish(w):
                pool.wait_ge(rec_ok, 4 * (w.n + 1))
                pool.wait_ge(mg_ok, element(w).n + 1)
                pool.tensor_tensor(rec[:], rec[:], mg[:, element(w).of(2), :], ALU.mult).then_inc(recm_ok, 1)
                pool.wait_ge(recm_ok, w.n + 1)
                pool.wait_ge(osb_ok, w.n + 1)
                pool.tensor_tensor(osb[:], osb[:], rec[:], ALU.mult).then_inc(out_ok, 1)
                pool.wait_ge(out_ok, w.n + 1)
                pool.wait_ge(xs_in[w.of(4)], 16 * GH * (w.use(4) + 1))
                at_least(pool, stored[w.of(2)], 16 * GH * w.use(2))
                pool.tensor_tensor(yo[:, w.of(2), :], osb[:], xs[:, w.of(4), :], ALU.add).then_inc(y_ok, 1)

            def step(t):
                a, b = t.u % GROUPS, element(t)
                if t.back(8).there:
                    finish(t.back(8))
                if not t.there:
                    return
                if a == 0:
                    pool.wait_ge(vare_ok, b.n + 1)
                    at_least(pool, xn_ok, b.n)
                    pool.tensor_tensor(rstd[:], vare[:], mhalf[:], ALU.pow).then_inc(rstd_ok, 1)
                if a == 1:
                    pool.wait_ge(xhi_ok, b.n + 1)
                    at_least(pool, piece_ok, PIECES * b.n)
                    pool.tensor_tensor(xn_lo[:], xn[:], xn_hi[:], ALU.subtract).then_inc(xlo_ok, 1)
                    pool.wait_ge(chi_ok, b.n + 1)
                    pool.tensor_tensor(cr_lo[:], cr[:], cr_hi[:], ALU.subtract).then_inc(clo_ok, 1)
                if a == 2:
                    for p in range(5):
                        if p < 4:
                            pool.wait_ge(proj_ok, 4 * b.n + p + 1)
                            pool.wait_ge(mask_in, 16 * (b.n + 1))
                            at_least(pool, plo_ok, 4 * b.n + p - 1)
                            pool.tensor_tensor(projm[:, p % 2, :], proj[:, p, :], mbc[:], ALU.mult).then_inc(projm_ok, 1)
                        if p > 0:
                            pool.wait_ge(phi_ok, 4 * b.n + p)
                            if p == 1:
                                at_least(pool, lay_ok, 16 * SPILLS * b.n)
                            pool.tensor_tensor(p_lo[:, p - 1, :], projm[:, (p - 1) % 2, :], p_hi[:, p - 1, :],
                                               ALU.subtract).then_inc(plo_ok, 1)

            roll(pool, step)

        @block.scalar
        def _(act):
            act.wait_ge(c_in, 64)
            act.activation(th[:], gt[:], ACT.Tanh).then_inc(tanh_ok, 1)
            act.activation(w_hi[:], raw, ACT.Copy).then_inc(whi_ok, 1)
            act.wait_ge(wlo_ok, 1)
            act.wait_ge(bq_ok, 1)

            def step(t):
                a, b = t.u % GROUPS, element(t)
                m, e, w = t.back(6), t.back(7), t.back(8)
                for j in range(8):
                    if j == 1 and w.there:
                        act.wait_ge(av_ok, TB * (w.n + 1))
                        at_least(act, y_ok, w.n)
                        act.activation(osb[:], psO[:], ACT.Copy).then_inc(osb_ok, 1)
                    if e.there:
                        act.wait_ge(b_ok, 8 * e.n + j + 1)
                        at_least(act, av_ok, 4 * e.n + j // 2 - 1)
                        act.activation(pt[:, j % 4], psB[j % 2][:], ACT.Exp).then_inc(exp_ok, 1)
                    if j == 0 and m.there:
                        act.wait_ge(mt_ok, m.n + 1)
                        at_least(act, max_in[m.of(2)], 16 * m.use(2))
                        act.activation(mrow[:, m.of(2), :], psM[0:GH, :], ACT.Copy).then_inc(mcopy_ok, 1)
                        act.wait_ge(mcopy_ok, m.n + 1)
                        act.dma_start(qs[MAX:MAX + 1, m.of(4), :, :].bitcast(F32),
                                      mrow[:, m.of(2), :].bitcast(F32)).then_inc(max_in[m.of(2)], 16)
                    if a == 2 and t.there and 2 <= j < 6:
                        p = j - 2
                        act.wait_ge(piece_ok, PIECES * b.n + p + 1)
                        at_least(act, projm_ok, 4 * b.n)
                        scale = 1.0 / HD ** 0.5 if p < 2 else 1.0
                        bias = bqk4 if p < 2 else bqk
                        act.activation(proj[:, p, :], psM[:], ACT.Identity, bias=bias[:, p:p + 1],
                                       scale=scale).then_inc(proj_ok, 1)
                    if a == 3 and t.there and j >= 4:
                        s = j - 4
                        act.wait_ge(vtmp_ok, 2 * b.n + s // 2 + 1)
                        act.wait_ge(mcol_in, 16 * (b.n + 1))
                        at_least(act, av_ok, 16 * (b.n - 1))
                        act.activation(va[:, b.of(2), s, :, 0:HD], vtmp[:, s // 2, s % 2, :].rearrange("p (h d) -> p h d", h=HEADS),
                                       ACT.Copy, scale=mcol[:, s:s + 1]).then_inc(v_ok, 1)

            roll(act, step)

        @block.tensor
        def _(pe):
            pe.wait_ge(ident_ok, 1)
            pe.wait_ge(wlo_ok, 1)
            pe.wait_ge(zero_ok, 4)

            def project(b, p):
                at_least(pe, mcopy_ok, 4 * b.n + p // 4 - 3)
                if p == 0:
                    pe.wait_ge(xlo_ok, b.n + 1)
                    pe.wait_ge(clo_ok, b.n + 1)
                if 1 <= p < 5:
                    pe.wait_ge(proj_ok, 4 * b.n + p)
                if p == 5:
                    pe.wait_ge(vtmp_ok, 2 * b.n + 1)
                if p < 4:
                    w, o = divmod(p, 2)
                    hi, lo = (xn_hi, xn_lo) if w == 0 else (cr_hi, cr_lo)
                    cols = slice(o * P, (o + 1) * P)
                    for k in range(KC):
                        for x, y in ((w_hi, hi), (w_hi, lo), (w_lo, hi)):
                            mm = pe.matmul(psM[:], x[:, w, k, cols], y[:, k, :], start=(k == 0 and x is w_hi and y is hi),
                                           stop=(k == KC - 1 and x is w_lo))
                else:
                    for s in range(2):
                        rows = slice(((p - 4) * 2 + s) * P, ((p - 4) * 2 + s + 1) * P)
                        for k in range(KC):
                            for x, y in ((cr_hi, w_hi), (cr_lo, w_hi), (cr_hi, w_lo)):
                                mm = pe.matmul(psM[:, s * C:(s + 1) * C], x[:, k, rows], y[:, 2, k, :],
                                               start=(k == 0 and x is cr_hi and y is w_hi), stop=(k == KC - 1 and y is w_lo))
                mm.then_inc(piece_ok, 1)

            def outputs(n, s):
                b, a = element(n), n.u % GROUPS
                pe.wait_ge(exp_ok, 8 * n.n + 2 * s + 2)
                if s == 0:
                    pe.wait_ge(v_ok, TB * (b.n + 1))
                    at_least(pe, osb_ok, n.n)
                for h in range(GH):
                    mm = pe.matmul(psO[32 * h:32 * h + 32, :], va[:, b.of(2), s, a * GH + h, :],
                                   pt[:, (2 * s + h // 2) % 4, h % 2, :], start=(s == 0), stop=(s == TB - 1))
                mm.then_inc(av_ok, 1)

            def step(t):
                a, b = t.u % GROUPS, element(t)
                s, m, e, w = t.back(5), t.back(6), t.back(7), t.back(8)
                for i in range(16):
                    if i == 1 and m.there:
                        pe.wait_ge(max_ok, 16 * (m.n + 1))
                        at_least(pe, mcopy_ok, m.n)
                        if a == 3 and t.there:
                            pe.wait_ge(proj_ok, 4 * (b.n + 1))
                        if a == 0 and t.back(1).there:
                            at_least(pe, vtmp_ok, 2 * b.n)
                        for k in range(TB):
                            mm = pe.transpose(psM[0:GH, k * P:(k + 1) * P], nmax[:, m.of(2), k, :], ident[:])
                        mm.then_inc(mt_ok, 1)
                    if s.there:
                        if i == 0:
                            pe.wait_ge(fill_in[s.of(4)], 32 * (s.use(4) + 1))
                        h, k = divmod(i, TB)
                        at_least(pe, max_ok, 16 * s.n + i - 1)
                        pe.matmul(psS[i % 2][:], qs[:, s.of(4), h, k * P:(k + 1) * P], ks[:, s.of(4), h, :],
                                  start=True, stop=True).then_inc(s_ok, 1)
                    if e.there:
                        if i == 0:
                            pe.wait_ge(max_in[e.of(2)], 16 * (e.use(2) + 1))
                        k, h = divmod(i, GH)
                        if i % 2 == 0:
                            at_least(pe, exp_ok, 8 * e.n + i // 2 - 1)
                        mm = pe.matmul(psB[i // 2 % 2][:, i % 2, :], ks[:, e.of(4), h, k * P:(k + 1) * P],
                                       qs[:, e.of(4), h, :], start=True, stop=True)
                        if i % 2:
                            mm.then_inc(b_ok, 1)
                    if i in (0, 3) and w.there:
                        outputs(w, 2 if i == 0 else 3)
                    if i in (8, 12) and e.there:
                        outputs(e, (i - 8) // 4)
                    if a == 2 and t.there and i in (3, 6, 9, 12):
                        project(b, (i - 3) // 3)
                    if a == 3 and t.there and i in (3, 8):
                        project(b, 4 + (i - 3) // 5)

            roll(pe, step)

        @block.vector
        def _(dve):
            dve.wait_ge(c_in, 64)
            dve.tensor_scalar(bqk4[:], bqk[:], 1.0 / HD ** 0.5, None, ALU.mult).then_inc(bq_ok, 1)
            dve.memset(va[:], 1.0).then_inc(zero_ok, 1)
            dve.wait_ge(mk_in, 16)
            q_rows, k_rows = qk[0:B, 3, 0], qk[0:B, 3, 1]
            dve.tensor_scalar(neg[:], mk[:], -1.0, NEG, ALU.add, ALU.mult).then_inc(mrow_ok, 1)
            dve.tensor_copy(q_rows[:, 0, :], mk[:]).then_inc(mrow_ok, 1)
            dve.tensor_copy(q_rows[:, 1, :], mk[:])
            dve.memset(q_rows[:, 3, :].bitcast(F32), 0.0).then_inc(mrow_ok, 1)
            dve.memset(k_rows[:, 3, :].bitcast(F32), 1.0).then_inc(mrow_ok, 1)
            dve.wait_ge(mrow_ok, 4)
            dve.tensor_tensor(q_rows[:, 2, :], mk[:], q_rows[:, 0, :], ALU.subtract).then_inc(mrow_ok, 1)
            dve.tensor_copy(k_rows[:, 0, :], neg[:]).then_inc(mrow_ok, 1)
            dve.tensor_copy(k_rows[:, 2, :], neg[:]).then_inc(mrow_ok, 1)
            dve.wait_ge(mrow_ok, 7)
            dve.tensor_tensor(k_rows[:, 1, :], neg[:], k_rows[:, 0, :], ALU.subtract).then_inc(mrow_ok, 1)
            dve.wait_ge(tanh_ok, 1)

            def finish(w):
                now, used = fixed(dve, w.n + 1), fixed(dve, 4 * w.n)
                dve.wait_ge(tanh_ok, 1)
                dve.wait_ge(osb_ok, now)
                at_least(dve, rec_ok, used)
                dve.stream_shuffle(den[:], osb[:], [HD + i % HD for i in range(32)]).then_inc(den_ok, 1)

            def step(t):
                a, b = t.u % GROUPS, element(t)
                s, w = t.back(5), t.back(8)
                for i in range(16):
                    if s.there:
                        h, k = divmod(i, TB)
                        dve.wait_ge(s_ok, 16 * s.n + i + 1)
                        at_least(dve, mt_ok, s.n - 1)
                        dve.tensor_reduce(nmax[:, s.of(2), k, h:h + 1], psS[i % 2][:], AX.X, ALU.max,
                                          negate=True).then_inc(max_ok, 1)
                    if i == 4 and w.there:
                        finish(w)
                    if 6 <= i < 10 and w.there:
                        cols = slice((i - 6) * P, (i - 5) * P)
                        dve.wait_ge(den_ok, w.n + 1)
                        at_least(dve, out_ok, w.n)
                        dve.reciprocal(rec[:, cols], den[:, cols]).then_inc(rec_ok, 1)
                    if not t.there:
                        continue
                    if a == 0 and i == 8:
                        dve.wait_ge(x_in, 16 * (b.n + 1))
                        for c in range(KC):
                            at_least(dve, mv_ok, KC * b.n)
                            dve.bn_stats(stats[:, c, :], xr[:, c, :]).then_inc(bn_ok, 1)
                    if a == 0 and i == 10:
                        for c in range(KC):
                            now, before = fixed(dve, KC * (b.n + 1)), fixed(dve, b.n)
                            dve.wait_ge(tanh_ok, 1)
                            dve.wait_ge(bn_ok, now)
                            at_least(dve, xn_ok, before)
                            dve.bn_aggr(mv[:, c, :], stats[:, c, :]).then_inc(mv_ok, 1)
                        dve.wait_ge(mv_ok, KC * (b.n + 1))
                        at_least(dve, rstd_ok, b.n)
                        dve.tensor_scalar(vare[:], mv[:, :, 1], EPS, None, ALU.add).then_inc(vare_ok, 1)
                    if a == 1 and i == 2:
                        dve.wait_ge(rstd_ok, b.n + 1)
                        at_least(dve, xlo_ok, b.n)
                        for c in range(KC):
                            mm = dve.tensor_scalar(xn[:, c, :], xr[:, c, :], mv[:, c, 0:1], rstd[:, c:c + 1],
                                                   ALU.subtract, ALU.mult)
                        mm.then_inc(xn_ok, 1)
                    if a == 1 and i == 4:
                        dve.wait_ge(xn_ok, b.n + 1)
                        at_least(dve, piece_ok, PIECES * b.n)
                        dve.tensor_copy(xn_hi[:], xn[:]).then_inc(xhi_ok, 1)
                        dve.wait_ge(ctx_in, 16 * (b.n + 1))
                        dve.tensor_copy(cr_hi[:], cr[:]).then_inc(chi_ok, 1)
                    if a == 3 and i == 10:
                        dve.wait_ge(mask_in, 16 * (b.n + 1))
                        at_least(dve, out_ok, 4 * (b.n - 1))
                        dve.tensor_scalar(mg[:, b.of(2), :], mbc[:], th[:, 0:1], None, ALU.mult).then_inc(mg_ok, 1)
                    if a == 2 and i in (10, 14) or a == 3 and i in (2, 6):
                        p = (0 if a == 2 else 2) + (i in (14, 6))
                        dve.wait_ge(projm_ok, 4 * b.n + p + 1)
                        if p == 0:
                            at_least(dve, lay_ok, 16 * SPILLS * b.n)
                        dve.tensor_copy(p_hi[:, p, :], projm[:, p % 2, :]).then_inc(phi_ok, 1)
                    if a == 3 and i in (5, 10):
                        r = (i - 5) // 5
                        dve.wait_ge(piece_ok, PIECES * b.n + 5 + r)
                        at_least(dve, v_ok, TB * b.n)
                        dve.tensor_tensor(vtmp[:, r], psM[:].rearrange("p (s c) -> p s c", s=2),
                                          bv[:].unsqueeze(1).broadcast_to((P, 2, C)), ALU.add).then_inc(vtmp_ok, 1)

            roll(dve, step)


def build(nc, x, ctx_t, ctx_rows, taps, skip, mask, mask_t, router, spread, moe_gu, moe_dn, w_qkv, b_qk, b_v,
          ffn_gu, ffn_dn, g, out):
    rows = [nc.dram_tensor(f"rows{i}", (C * B, L), F32, kind="Internal").ap() for i in range(3)]
    taps_pad = nc.dram_tensor("taps_pad", (32, L + P), F32, kind="Internal").ap()
    group = lambda a: lambda n: a[bass.ds(n * 1024, 1024), :].rearrange("(t p) d -> p t d", p=P)
    mix_phase(nc, x, ctx_t, taps, skip, g[0], taps_pad, rows[0])
    ffn_phase(nc, "moe", group(rows[0]), group(rows[1]), moe_gu, moe_dn, 5, 3, g[1], 8, router, spread)
    attention_phase(nc, rows[1], ctx_rows, mask, mask_t, w_qkv, b_qk, b_v, g[2], rows[2])
    ffn_phase(nc, "ffn", group(rows[2]), group(out), ffn_gu, ffn_dn, 1, 4, g[3])


def kernel(**inputs):
    import numpy as np
    import concourse.bacc as bacc
    from concourse.bass_utils import run_bass_kernel_spmd

    a = {k: np.asarray(v) for k, v in inputs.items()}
    x, c = a["x"], a["ctx_2048"]
    mask = a["mask_Bx1x2048_fk1"].reshape(B, L)
    pair = lambda w: w.reshape(4, 2, 512, 192).transpose(0, 2, 1, 3).reshape(4, 512, 384)
    gate = np.concatenate([pair(a["L0_ffn_w_gate"]), a["L0_ffn_shared_gate"][None]])
    up = np.concatenate([pair(a["L0_ffn_w_up"]), a["L0_ffn_shared_up"][None]])
    down = np.concatenate([a["L0_ffn_w_down"].reshape(4, 384, 512), a["L0_ffn_shared_down"][None]])
    spread = np.zeros((5, P, 384), np.float32)
    for u in range(5):
        for f in range(384):
            e = 8 if u == 4 else 2 * u + f // 192
            spread[u, e, f] = spread[u, 32 + e, f] = 1.0
    turn = lambda w: w.reshape(w.shape[:-1] + (2, 8, 16)).swapaxes(-1, -2).reshape(w.shape)
    wq, wk, wv = (f(a[f"L1_xattn_W{n}"].T).reshape(2, P, C) for n, f in (("q", turn), ("k", turn), ("v", lambda w: w)))
    bq, bk = (turn(a[f"L1_xattn_b{n}"]).reshape(2, P) for n in "qk")
    g = np.stack([a["g_xattn"][0], a["g_ffn"][0], a["g_xattn"][1], a["g_ffn"][1]])
    arrays = {
        "x": x.transpose(1, 0, 2).reshape(C * B, L),
        "ctx_t": c.reshape(B, 32, 8, 4, P)[..., ::-1].transpose(1, 4, 3, 2, 0).reshape(32, P, 4, P),
        "ctx_rows": c,
        "taps": a["L0_xattn_ssm_kernel"],
        "skip": a["L0_xattn_D"].reshape(32, 1),
        "mask": mask,
        "mask_t": mask.reshape(B, 4, P).transpose(0, 2, 1),
        "router": a["L0_ffn_router"].reshape(4, P, 8).transpose(1, 0, 2),
        "spread": spread,
        "moe_gu": np.concatenate([gate, up], 2).reshape(5, 4, P, 768).transpose(0, 2, 1, 3),
        "moe_dn": down.reshape(5, 3, P, 512).transpose(0, 2, 1, 3),
        "w_qkv": np.stack([wq, wk, wv]).transpose(2, 0, 1, 3),
        "b_qk": np.stack([bq[0], bq[1], bk[0], bk[1]], 1),
        "b_v": a["L1_xattn_bv"].reshape(1, C),
        "ffn_gu": a["L1_ffn_gate_up_proj"].reshape(4, 4, P, 1024).transpose(0, 2, 1, 3),
        "ffn_dn": a["L1_ffn_down_proj"].reshape(4, 4, P, 512).transpose(0, 2, 1, 3),
        "g": np.broadcast_to(g[:, None, None], (4, P, 1)),
    }
    arrays = {f"in_{k}": np.ascontiguousarray(v) for k, v in arrays.items()}
    nc = bacc.Bacc("TRN2", target_bir_lowering=False, num_devices=1)
    args = [nc.dram_tensor(k, v.shape, mybir.dt.from_np(v.dtype), kind="ExternalInput").ap() for k, v in arrays.items()]
    out = nc.dram_tensor("out_rows", (C * B, L), F32, kind="ExternalOutput").ap()
    build(nc, *args, out)
    r = run_bass_kernel_spmd(nc, [arrays], core_ids=[0])
    y = r.results[0]["out_rows"].reshape(4, C // 4, B, L)
    return np.ascontiguousarray(y.transpose(2, 1, 0, 3)).reshape(B, C, L)
```

```python
from contextlib import ExitStack, contextmanager
import concourse.bass as bass
from concourse import mybir
from concourse.alu_op_type import AluOpType as ALU
F32=mybir.dt.float32; F32R=mybir.dt.float32r
ACT=mybir.ActivationFunctionType; AX=mybir.AxisListType

P = 128
B = 16
C = 256
L = 512
EPS = 1e-5


class At:

    def __init__(self, k, u, unroll, count):
        k, u = k + u // unroll, u % unroll
        self.k, self.u, self.unroll, self.count = k, u, unroll, count
        self.n = unroll * k + u

    def back(self, d):
        return At(self.k, self.u - d, self.unroll, self.count)

    @property
    def there(self):
        return not isinstance(self.n, int) or 0 <= self.n < self.count

    def first(self, m):
        return isinstance(self.n, int) and self.n < m

    def of(self, m):
        return self.u % m

    def use(self, m):
        return (self.unroll // m) * self.k + self.u // m


def rolled(eng, step, count, unroll, lag):
    for u in range(unroll):
        step(At(0, u, unroll, count))
    with eng.Fori(1, count // unroll, 1) as k:
        for u in range(unroll):
            step(At(k, u, unroll, count))
    for u in range(lag):
        step(At(count // unroll, u, unroll, count))


def at_least(eng, sem, value):
    if not isinstance(value, int) or value > 0:
        eng.wait_ge(sem, value)


def fixed(eng, value, size=1):
    if not isinstance(value, int):
        eng.lower_val(value)
        if size > 1:
            eng.lower_val(value * size)
    return value


@contextmanager
def semaphores(nc, prefix):
    made = []

    def sem(name):
        made.append(nc.alloc_semaphore(name=f"{prefix}_{name}"))
        return made[-1]

    yield sem
    nc.all_engine_barrier()
    nc.clear_and_free_semaphores(made)
    nc.all_engine_barrier()


def mix_phase(nc, x_rows, ctx_t, taps_in, skip_in, g, taps_pad, x1):
    HEADS = 32
    HD = C // HEADS
    LB = L // P
    PAIRW = HD * B
    HALF = 2 * PAIRW + 2 * B
    SLOTW = (HD + 3) * B
    HALVED = 3
    PADW = L + P
    with ExitStack() as ctx:
        sb = lambda n, s, d=F32: ctx.enter_context(nc.sbuf_tensor(n, s, d))
        sem = ctx.enter_context(semaphores(nc, "mix"))
        pad = sb("pad", [HEADS, PADW])
        skip = sb("skip", [HEADS, 1])
        xr = sb("xr", [P, 4, L])
        cT = sb("cT", [P, 2, LB, HD + 3, B])
        skew = sb("skew", [P, 2, L])
        kv = sb("kv", [P, 2, LB, 2, HALF])
        stats = sb("stats", [P, 6])
        mv = sb("mv", [P, 2, 2])
        vare = sb("vare", [P, 1])
        mhalf = sb("mhalf", [P, 1])
        rstd = sb("rstd", [P, 1])
        xn = sb("xn", [P, L])
        qq = sb("qq", [P, 2, LB, 2 * PAIRW])
        z = sb("z", [P, LB, 8, SLOTW])
        zs = sb("zs", [P, HALVED, 4, SLOTW])
        o = sb("o", [P, 2, LB, SLOTW])
        y1 = sb("y1", [P, 2, L])
        ident = sb("ident", [P, P])
        gt = sb("gt", [P, 1])
        th = sb("th", [P, 1])
        psY = [ctx.enter_context(nc.psum_tensor(f"psY{i}", [P, 2, 512], F32)) for i in range(3)]
        psQ = ctx.enter_context(nc.psum_tensor("psQ", [P, L], F32))
        psO = ctx.enter_context(nc.psum_tensor("psO", [P, L], F32))

        skip_in_ok = sem("skip_in"); g_in_ok = sem("g_in"); taps_in_ok = sem("taps_in")
        pad_zero = sem("pad_zero"); pad_ok = sem("pad_ok"); pad_out = sem("pad_out")
        ident_zero = sem("ident_zero"); ident_ok = sem("ident_ok"); z_zero = sem("z_zero")
        mhalf_ok = sem("mhalf_ok"); tanh_ok = sem("tanh_ok")
        bn_ok = sem("bn_ok"); mv_ok = sem("mv_ok"); vare_ok = sem("vare_ok")
        rstd_ok = sem("rstd_ok"); xn_ok = sem("xn_ok"); qt_ok = sem("qt_ok")
        qq_ok = sem("qq_ok"); kv_ok = sem("kv_ok"); conv_ok = sem("conv_ok")
        z_ok = sem("z_ok"); half_ok = sem("half_ok"); sum_ok = sem("sum_ok"); wrap_ok = sem("wrap_ok")
        ot_ok = sem("ot_ok"); y1_ok = sem("y1_ok")
        x_in = [sem(f"x_in{u}") for u in range(4)]
        c_in = [sem(f"c_in{u}") for u in range(2)]
        skew_in = [sem(f"skew_in{u}") for u in range(2)]
        stored = [sem(f"stored{u}") for u in range(2)]
        block = ctx.enter_context(nc.Block())
        roll = lambda eng, step: rolled(eng, step, HEADS, 4, 2)
        buffer, last_use = (0, 1, 2, 0, 1, 2, 0, 1), (2, 2, 5, 3, 3, 3, 3, 3)

        @block.sync
        def _(sp):
            sp.wait_ge(pad_zero, 1)
            sp.dma_start(pad[:, P - 1:P - 1 + L], taps_in).then_inc(taps_in_ok, 16)
            sp.dma_start(skip[:], skip_in).then_inc(skip_in_ok, 16)
            sp.dma_start(gt[:], g).then_inc(g_in_ok, 16)
            sp.wait_ge(pad_ok, 1)
            sp.dma_start(taps_pad, pad[:]).then_inc(pad_out, 16)
            sp.wait_ge(pad_out, 16)

            def load(t):
                if not t.there:
                    return
                if not t.first(4):
                    sp.wait_ge(y1_ok, t.n - 3)
                sp.dma_start(xr[:, t.of(4), :], x_rows[bass.ds(t.n * P, P), :]).then_inc(x_in[t.of(4)], 16)
                if not t.first(2):
                    sp.wait_ge(kv_ok, 3 * (t.n - 1))
                src = ctx_t[bass.ds(t.n, 1)].rearrange("o p l w -> (o p) l w")
                dst = cT[:, t.of(2)].rearrange("p l i b -> p l (i b)")
                sp.dma_start(dst[:, :, 0:PAIRW], src).then_inc(c_in[t.of(2)], 16)
                sp.dma_start(dst[:, :, PAIRW:], src[:, :, 0:3 * B]).then_inc(c_in[t.of(2)], 16)
                if not t.first(2):
                    sp.wait_ge(conv_ok, LB * (t.n - 1))
                sp.dma_start(skew[:, t.of(2), :], bass.AP(tensor=taps_pad.tensor, offset=t.n * PADW,
                                                          ap=[[1, P], [1, L]])).then_inc(skew_in[t.of(2)], 16)

            roll(sp, load)

        @block.gpsimd
        def _(pool):
            pool.memset(pad[:], 0.0).then_inc(pad_zero, 1)
            pool.memset(ident[:], 0.0).then_inc(ident_zero, 1)
            pool.memset(mhalf[:], -0.5).then_inc(mhalf_ok, 1)
            pool.wait_ge(ident_zero, 1)
            pool.affine_select(out=ident[:], in_=ident[:], compare_op=ALU.not_equal, fill=1.0, base=0,
                               pattern=[[-1, P]], channel_multiplier=1).then_inc(ident_ok, 1)
            pool.memset(z[:], 0.0).then_inc(z_zero, 1)
            pool.wait_ge(mhalf_ok, 1)

            def half_sums(h, ob):
                pool.wait_ge(z_ok, 4 * (LB * h.n + ob + 1))
                if not h.first(1):
                    pool.wait_ge(sum_ok, LB * (h.n - 1) + ob + 1)
                pool.tensor_tensor(zs[:, ob], z[:, ob, 0:4, :], z[:, ob, 4:8, :], ALU.add).then_inc(half_ok, 1)

            def step(t):
                h, u = t.back(1), t.of(2)
                if t.there:
                    pool.wait_ge(vare_ok, t.n + 1)
                    if not t.first(1):
                        pool.wait_ge(xn_ok, t.n)
                    pool.tensor_tensor(rstd[:], vare[:], mhalf[:], ALU.pow).then_inc(rstd_ok, 1)
                    pool.wait_ge(c_in[u], 32 * (t.use(2) + 1))
                    if not t.first(2):
                        pool.wait_ge(conv_ok, LB * (t.n - 1))
                c = cT[:, u].rearrange("p l i b -> p l (i b)")
                for r in range(3):
                    if t.there and r < 2:
                        one = c[:, :, 0:PAIRW].unsqueeze(2).broadcast_to((P, LB, 2, PAIRW))
                        base = c[:, :, 2 * r * B:2 * r * B + PAIRW]
                        other = bass.AP(tensor=base.tensor, offset=base.offset,
                                        ap=[list(base.ap[0]), [SLOTW, LB], [B, 2], [1, PAIRW]])
                        out = kv[:, u, :, r, 0:2 * PAIRW].rearrange("p l (r w) -> p l r w", r=2)
                        pool.tensor_tensor(out, one, other, ALU.mult).then_inc(kv_ok, 1)
                    elif t.there:
                        pool.tensor_tensor(kv[:, u, :, :, 2 * PAIRW:],
                                           c[:, :, 0:4 * B].rearrange("p l (h w) -> p l h w", h=2),
                                           c[:, :, 4 * B:8 * B].rearrange("p l (h w) -> p l h w", h=2),
                                           ALU.mult).then_inc(kv_ok, 1)
                    if h.there:
                        half_sums(h, r)

            roll(pool, step)

        @block.scalar
        def _(act):
            act.wait_ge(g_in_ok, 16)
            act.activation(th[:], gt[:], ACT.Tanh).then_inc(tanh_ok, 1)
            act.wait_ge(tanh_ok, 1)

            def step(t):
                if t.there:
                    act.wait_ge(qt_ok, t.n + 1)
                    if not t.first(2):
                        act.wait_ge(z_ok, 4 * LB * (t.n - 1))
                    src = psQ[:].rearrange("p (l w) -> p l w", l=LB)
                    for c in range(2):
                        act.activation(qq[:, t.of(2), :, c * PAIRW:(c + 1) * PAIRW], src, ACT.Copy,
                                       scale=th[:, 0:1]).then_inc(qq_ok, 1)
                t = t.back(2)
                if t.there:
                    act.wait_ge(y1_ok, t.n + 1)
                    act.dma_start(x1[bass.ds(t.n * P, P), :], y1[:, t.of(2), :]).then_inc(stored[t.of(2)], 16)

            roll(act, step)
            for u in range(2):
                act.wait_ge(stored[u], 16 * (HEADS // 2))

        @block.tensor
        def _(pe):
            pe.wait_ge(ident_ok, 1)

            def step(t):
                a, h, w = t, t.back(1), t.back(2)
                for ob in range(LB):
                    if ob == 3 and a.there:
                        pe.wait_ge(xn_ok, a.n + 1)
                        if not a.first(1):
                            pe.wait_ge(qq_ok, 2 * a.n)
                        for l in range(LB):
                            mm = pe.transpose(psQ[:, l * P:(l + 1) * P], xn[:, l * P:(l + 1) * P], ident[:])
                        mm.then_inc(qt_ok, 1)
                    if h.there:
                        u = h.of(2)
                        if ob == 0:
                            pe.wait_ge(kv_ok, 3 * (h.n + 1))
                            pe.wait_ge(skew_in[u], 16 * (h.use(2) + 1))
                        at = (LB * h.u + ob) % 8
                        i = buffer[at]
                        at_least(pe, z_ok, 4 * (LB * h.n + ob + 1 - last_use[at]))
                        for m in range(ob + 1):
                            for half in range(2):
                                mm = pe.matmul(psY[i][:, half, 0:HALF], skew[:, u, (ob - m) * P:(ob - m + 1) * P],
                                               kv[:, u, m, half, :], start=(m == 0), stop=(m == ob))
                        mm.then_inc(conv_ok, 1)
                if w.there:
                    pe.wait_ge(wrap_ok, w.n + 1)
                    if not w.first(1):
                        pe.wait_ge(y1_ok, w.n)
                    for l in range(LB):
                        mm = pe.transpose(psO[:, l * P:(l + 1) * P], o[:, w.of(2), l, 0:PAIRW], ident[:])
                    mm.then_inc(ot_ok, 1)

            roll(pe, step)

        @block.vector
        def _(dve):
            dve.wait_ge(taps_in_ok, 16)
            dve.wait_ge(skip_in_ok, 16)
            dve.tensor_tensor(pad[:, P - 1:P], pad[:, P - 1:P], skip[:], ALU.add).then_inc(pad_ok, 1)
            dve.wait_ge(z_zero, 1)

            def sums(h, ob):
                now = LB * h.n + ob + 1
                if ob < HALVED:
                    dve.wait_ge(half_ok, HALVED * h.n + ob + 1)
                else:
                    dve.wait_ge(z_ok, 4 * now)
                if ob == 0 and not h.first(2):
                    dve.wait_ge(ot_ok, h.n - 1)
                dve.tensor_reduce(o[:, h.of(2), ob], (zs if ob < HALVED else z)[:, ob].rearrange("p s w -> p w s"), AX.X,
                                  ALU.add).then_inc(sum_ok, 1)
                if ob == LB - 1:
                    dve.wait_ge(sum_ok, now)
                    oo = o[:, h.of(2)]
                    dve.tensor_tensor(oo[:, :, 0:3 * B], oo[:, :, 0:3 * B], oo[:, :, PAIRW:], ALU.add).then_inc(wrap_ok, 1)

            def step(t):
                a, h, w = t, t.back(1), t.back(2)
                if a.there:
                    dve.wait_ge(x_in[a.of(4)], 16 * (a.use(4) + 1))
                    if not a.first(1):
                        dve.wait_ge(mv_ok, a.n)
                    dve.bn_stats(stats[:], xr[:, a.of(4), :]).then_inc(bn_ok, 1)
                    now, before = fixed(dve, a.n + 1), fixed(dve, a.n - 1)
                    dve.wait_ge(pad_ok, 1)
                    dve.wait_ge(bn_ok, now)
                    if not a.first(2):
                        dve.wait_ge(xn_ok, before)
                    dve.bn_aggr(mv[:, a.of(2), :], stats[:]).then_inc(mv_ok, 1)
                    dve.wait_ge(mv_ok, a.n + 1)
                    if not a.first(1):
                        dve.wait_ge(rstd_ok, a.n)
                    dve.tensor_scalar(vare[:], mv[:, a.of(2), 1:2], EPS, None, ALU.add).then_inc(vare_ok, 1)
                for ob in range(LB):
                    if ob == 1 and a.there:
                        dve.wait_ge(rstd_ok, a.n + 1)
                        if not a.first(1):
                            dve.wait_ge(qt_ok, a.n)
                        dve.tensor_scalar(xn[:], xr[:, a.of(4), :], mv[:, a.of(2), 0:1], rstd[:, 0:1],
                                          ALU.subtract, ALU.mult).then_inc(xn_ok, 1)
                    if h.there:
                        if ob == 0:
                            dve.wait_ge(qq_ok, 2 * (h.n + 1))
                            if not h.first(1):
                                dve.wait_ge(half_ok, HALVED * h.n)
                        if ob == LB - 1 and not h.first(1):
                            dve.wait_ge(sum_ok, LB * h.n)
                        dve.wait_ge(conv_ok, LB * h.n + ob + 1)
                        y = psY[buffer[(LB * h.u + ob) % 8]]
                        q = qq[:, h.of(2), ob, :]
                        zz = z[:, ob]

                        def shifted(base, dims):
                            return bass.AP(tensor=base.tensor, offset=base.offset, ap=[list(base.ap[0])] + dims)
                        dve.tensor_tensor(
                            shifted(zz, [[2 * SLOTW, 2], [SLOTW, 2], [1, PAIRW]]),
                            y[:, :, 0:2 * PAIRW].rearrange("p h (r w) -> p h r w", r=2),
                            shifted(q, [[2 * B, 2], [B, 2], [1, PAIRW]]), ALU.mult).then_inc(z_ok, 1)
                        dve.tensor_tensor(
                            shifted(zz[:, 4, :], [[4 * B, 2], [2 * B, 2], [1, 2 * B]]),
                            y[:, :, 2 * PAIRW:HALF].unsqueeze(1).broadcast_to((P, 2, 2, 2 * B)),
                            shifted(q[:, 4 * B:], [[4 * B, 2], [2 * B, 2], [1, 2 * B]]), ALU.mult).then_inc(z_ok, 1)
                        dve.tensor_tensor(zz[:, 5, B:B + PAIRW], y[:, 0, PAIRW:2 * PAIRW], q[:, 0:PAIRW],
                                          ALU.mult).then_inc(z_ok, 1)
                        dve.tensor_tensor(
                            shifted(zz[:, 6, 2 * B:], [[SLOTW + B, 2], [1, PAIRW]]),
                            y[:, 1, 0:2 * PAIRW].rearrange("p (r w) -> p r w", r=2),
                            q[:, 0:PAIRW].unsqueeze(1).broadcast_to((P, 2, PAIRW)), ALU.mult).then_inc(z_ok, 1)
                    if ob < 2 and w.there:
                        sums(w, ob + 2)
                    if ob >= 2 and h.there:
                        sums(h, ob - 2)
                if w.there:
                    dve.wait_ge(ot_ok, w.n + 1)
                    if not w.first(2):
                        dve.wait_ge(stored[w.of(2)], 16 * w.use(2))
                    dve.tensor_tensor(y1[:, w.of(2), :], psO[:], xr[:, w.of(4), :], ALU.add).then_inc(y1_ok, 1)

            roll(dve, step)


def ffn_phase(nc, name, load_rows, store_rows, w_gu, w_dn, units, FC, g, experts=0, router=None, spread=None):
    TOP_K = 2
    GROUPS, T = 4, 8
    KD = L // P
    HALVES = T * P // 512
    TH = T // HALVES
    F = FC * P
    CH = HALVES * FC
    GATE = experts > 0
    with ExitStack() as ctx:
        sb = lambda n, s, d=F32: ctx.enter_context(nc.sbuf_tensor(f"{name}_{n}", s, d))
        sem = ctx.enter_context(semaphores(nc, name))
        ps = lambda n, s: ctx.enter_context(nc.psum_tensor(f"{name}_{n}", s, F32))
        xg = sb("xg", [P, 2, T, L])
        stats = sb("stats", [P, T, 6]); mv = sb("mv", [P, T, 2])
        vare = sb("vare", [P, T]); mhalf = sb("mhalf", [P, T]); rstd = sb("rstd", [P, T])
        xn = sb("xn", [P, 2, L])
        zhi = sb("zhi", [P, KD, T * P], F32R); zlo = sb("zlo", [P, KD, T * P], F32R)
        gu_raw = sb("gu_raw", [P, KD, 2 * F]); dn_raw = sb("dn_raw", [P, FC, L])
        gu_hi = sb("gu_hi", [P, KD, 2 * F], F32R); gu_lo = sb("gu_lo", [P, KD, 2 * F], F32R)
        dn_hi = sb("dn_hi", [P, FC, L], F32R); dn_lo = sb("dn_lo", [P, FC, L], F32R)
        act_g = sb("act_g", [P, 2, 512]); hid = sb("hid", [P, 2, 512])
        h_hi = sb("h_hi", [P, FC, T * P], F32R); h_lo = sb("h_lo", [P, FC, T * P], F32R)
        ident = sb("ident", [P, P]); gt = sb("gt", [P, 1]); th = sb("th", [P, 1])
        psG = [ps(f"psG{i}", [P, 512]) for i in range(2)]
        psU = [ps(f"psU{i}", [P, 512]) for i in range(2)]
        psD = [ps(f"psD{i}", [P, 512]) for i in range(2)]
        psC = ps("psC", [P, 512])
        psT = ps("psT", [P, 512])
        psP = [psT, psC]

        x_in = [sem(f"x_in{i}") for i in range(2)]; g_in = sem("g_in"); gu_in = sem("gu_in"); dn_in = sem("dn_in")
        ident_zero = sem("ident_zero"); ident_ok = sem("ident_ok"); mhalf_ok = sem("mhalf_ok"); tanh_ok = sem("tanh_ok")
        bn_ok = sem("bn_ok"); mv_ok = sem("mv_ok"); vare_ok = sem("vare_ok"); rstd_ok = sem("rstd_ok")
        xn_ok = sem("xn_ok"); zt_ok = sem("zt_ok"); zhi_ok = sem("zhi_ok"); zlo_ok = sem("zlo_ok")
        guhi_ok = sem("guhi_ok"); gulo_ok = sem("gulo_ok"); dnhi_ok = sem("dnhi_ok"); dnlo_ok = sem("dnlo_ok")
        gate_ok = sem("gate_ok"); up_ok = sem("up_ok"); silu_ok = sem("silu_ok")
        hid_ok = sem("hid_ok"); hhi_ok = sem("hhi_ok"); hlo_ok = sem("hlo_ok")
        down_ok = sem("down_ok"); acc_ok = sem("acc_ok"); stored = sem("stored")
        if GATE:
            hid2 = sb("hid2", [P, 2, 512])
            r_raw = sb("r_raw", [P, KD, P]); r_hi = sb("r_hi", [P, KD, P], F32R); r_lo = sb("r_lo", [P, KD, P], F32R)
            spread_raw = sb("spread_raw", [P, F]); spread_r = sb("spread_r", [P, F], F32R)
            lgT = sb("lgT", [P, 512]); lg = sb("lg", [P, T, experts]); ex = sb("ex", [P, T, experts])
            mx = sb("mx", [P, T]); den = sb("den", [P, T]); rden = sb("rden", [P, T])
            above = sb("above", [P, T, experts, experts]); same = sb("same", [P, T, experts, experts])
            lower = sb("lower", [P, experts, experts]); rank = sb("rank", [P, T, experts]); pick = sb("pick", [P, T, experts])
            cw = sb("cw", [P, T, P]); cwT = sb("cwT", [P, T * P], F32R)
            r_in = sem("r_in"); rz_ok = sem("rz_ok"); rhi_ok = sem("rhi_ok"); rlo_ok = sem("rlo_ok")
            spread_in = sem("spread_in"); spread_ok = sem("spread_ok")
            lgt_ok = sem("lgt_ok"); lgs_ok = sem("lgs_ok"); lgb_ok = sem("lgb_ok"); lg_ok = sem("lg_ok")
            sm_ok = sem("sm_ok"); exp_ok = sem("exp_ok"); rank_ok = sem("rank_ok"); low0_ok = sem("low0_ok"); lower_ok = sem("lower_ok")
            cw0_ok = sem("cw0_ok"); cw_ok = sem("cw_ok"); cwt_ok = sem("cwt_ok"); cwhi_ok = sem("cwhi_ok"); cwlo_ok = sem("cwlo_ok")
            cwb_ok = sem("cwb_ok"); hid2_ok = sem("hid2_ok")
        block = ctx.enter_context(nc.Block())
        src_h, src_ok = (hid2, hid2_ok) if GATE else (hid, hid_ok)

        def each_group(eng, hidden, boundary):
            for grp in range(GROUPS):
                boundary(grp * units, grp, grp - 1)
                hidden(grp * units, grp + 1 if units == 1 else None)
                if units > 1:
                    with eng.Fori(1, units - 1, 1) as un:
                        boundary(grp * units + un, None, grp)
                        hidden(grp * units + un, None)
                    boundary(grp * units + units - 1, None, grp)
                    hidden(grp * units + units - 1, grp + 1)
            boundary(GROUPS * units, GROUPS, GROUPS - 1)

        @block.sync
        def _(sp):
            sp.dma_start(gt[:], g).then_inc(g_in, 16)
            if GATE:
                sp.wait_ge(rz_ok, 1)
                sp.dma_start(r_raw[:, :, 0:experts], router).then_inc(r_in, 16)

            def weights(n, un):
                at_least(sp, gulo_ok, KD * n)
                sp.dma_start(gu_raw[:], w_gu[bass.ds(un, 1)].rearrange("o p k f -> (o p) k f")).then_inc(gu_in, 16)
                if GATE:
                    at_least(sp, spread_ok, n)
                    sp.dma_start(spread_raw[:], spread[bass.ds(un, 1)].rearrange("o p f -> (o p) f")).then_inc(spread_in, 16)
                at_least(sp, dnlo_ok, n)
                sp.dma_start(dn_raw[:], w_dn[bass.ds(un, 1)].rearrange("o p k f -> (o p) k f")).then_inc(dn_in, 16)

            def load(grp):
                if grp >= 2:
                    sp.wait_ge(stored, 16 * (grp - 1))
                sp.dma_start(xg[:, grp % 2], load_rows(grp)).then_inc(x_in[grp % 2], 16)

            def store(grp):
                sp.wait_ge(acc_ok, T * units * (grp + 1))
                sp.dma_start(store_rows(grp), xg[:, grp % 2]).then_inc(stored, 16)

            load(0)
            for grp in range(GROUPS):
                if GATE:
                    weights(grp * units, 0)
                    with sp.Fori(1, units, 1) as un:
                        weights(grp * units + un, un)
                else:
                    weights(grp, grp)
                if grp > 0:
                    store(grp - 1)
                if grp + 1 < GROUPS:
                    load(grp + 1)
            store(GROUPS - 1)
            sp.wait_ge(stored, 16 * GROUPS)

        @block.gpsimd
        def _(pool):
            pool.memset(ident[:], 0.0).then_inc(ident_zero, 1)
            pool.memset(mhalf[:], -0.5).then_inc(mhalf_ok, 1)
            if GATE:
                pool.memset(r_raw[:], 0.0).then_inc(rz_ok, 1)
                pool.memset(cwT[:].bitcast(F32), 0.0).then_inc(cw0_ok, 1)
                pool.memset(cw[:], 1.0).then_inc(cw0_ok, 1)
                pool.memset(lower[:], 1.0).then_inc(low0_ok, 1)
                pool.wait_ge(low0_ok, 1)
                pool.affine_select(out=lower[:], in_=lower[:], compare_op=ALU.is_gt, fill=0.0, base=0,
                                   pattern=[[1, experts], [-1, experts]], channel_multiplier=0).then_inc(lower_ok, 1)
            pool.wait_ge(ident_zero, 1)
            pool.affine_select(out=ident[:], in_=ident[:], compare_op=ALU.not_equal, fill=1.0, base=0,
                               pattern=[[-1, P]], channel_multiplier=1).then_inc(ident_ok, 1)
            pool.wait_ge(mhalf_ok, 1)
            for grp in range(GROUPS):
                pool.wait_ge(vare_ok, grp + 1)
                at_least(pool, xn_ok, T * grp)
                pool.tensor_tensor(rstd[:], vare[:], mhalf[:], ALU.pow).then_inc(rstd_ok, 1)

        @block.scalar
        def _(act):
            act.wait_ge(g_in, 16)
            act.activation(th[:], gt[:], ACT.Tanh).then_inc(tanh_ok, 1)
            if GATE:
                act.wait_ge(r_in, 16)
                act.activation(r_hi[:], r_raw[:], ACT.Copy).then_inc(rhi_ok, 1)
                act.wait_ge(cw0_ok, 2)

            def tile(grp, t):
                act.wait_ge(zt_ok, T * grp + t + 1)
                at_least(act, up_ok, CH * units * grp)
                act.activation(zhi[:, :, t * P:(t + 1) * P], psP[t % 2][:].rearrange("p (k w) -> p k w", k=KD),
                               ACT.Copy).then_inc(zhi_ok, 1)

            def route(grp):
                for h in range(HALVES):
                    act.wait_ge(lgt_ok, HALVES * grp + h + 1)
                    at_least(act, lgb_ok, HALVES * grp + h)
                    act.activation(lgT[:], psT[:], ACT.Copy).then_inc(lgs_ok, 1)
                act.wait_ge(sm_ok, 4 * grp + 2)
                at_least(act, cw_ok, grp)
                act.activation(ex[:], lg[:], ACT.Exp).then_inc(exp_ok, 1)
                for h in range(HALVES):
                    act.wait_ge(cwt_ok, HALVES * grp + h + 1)
                    at_least(act, cwb_ok, CH * units * grp)
                    act.activation(cwT[0:32, h * 512:(h + 1) * 512], psP[h][0:32, :], ACT.Copy).then_inc(cwhi_ok, 1)

            def boundary(n, grp, current):
                for t in range(T):
                    if t % 2 == 0 and grp != GROUPS:
                        k = t // 2
                        if k == 0:
                            act.wait_ge(gu_in, 16 * n + 16)
                            at_least(act, up_ok, CH * n)
                        at_least(act, gulo_ok, KD * n - KD + k + 1)
                        act.activation(gu_hi[:, k, :], gu_raw[:, k, :], ACT.Copy).then_inc(guhi_ok, 1)
                    if grp is not None and grp < GROUPS:
                        tile(grp, t)
                if grp == GROUPS:
                    return
                if GATE:
                    act.wait_ge(spread_in, 16 * n + 16)
                    act.activation(spread_r[:], spread_raw[:], ACT.Copy).then_inc(spread_ok, 1)
                if GATE and grp is not None:
                    route(grp)
                act.wait_ge(dn_in, 16 * n + 16)
                at_least(act, down_ok, T * n)
                at_least(act, dnlo_ok, n)
                act.activation(dn_hi[:], dn_raw[:], ACT.Copy).then_inc(dnhi_ok, 1)

            def hidden(n, ahead):
                for i in range(CH + 1):
                    j = CH * n + i
                    if i < CH:
                        act.wait_ge(gate_ok, j + 1)
                        act.wait_ge(hid_ok, j - 1 if i else j)
                        act.activation(act_g[:, i % 2, :], psG[i % 2][:], ACT.Silu).then_inc(silu_ok, 1)
                    if i > 0:
                        h, c = divmod(i - 1, FC)
                        act.wait_ge(src_ok, j)
                        act.wait_ge(down_ok, T * n)
                        act.activation(h_hi[:, c, h * 512:(h + 1) * 512], src_h[:, (i - 1) % 2, :],
                                       ACT.Copy).then_inc(hhi_ok, 1)

            each_group(act, hidden, boundary)

        @block.tensor
        def _(pe):
            pe.wait_ge(ident_ok, 1)

            def tile(grp, t):
                pe.wait_ge(xn_ok, T * grp + t + 1)
                at_least(pe, zlo_ok, T * grp + t - 1 if t >= 2 else T * grp)
                if GATE and t < 2:
                    at_least(pe, hid2_ok, CH * units * grp)
                    at_least(pe, cwlo_ok, HALVES * grp)
                for k in range(KD):
                    mm = pe.transpose(psP[t % 2][:, k * P:(k + 1) * P], xn[:, t % 2, k * P:(k + 1) * P], ident[:])
                mm.then_inc(zt_ok, 1)

            def route(grp):
                if grp == 0:
                    pe.wait_ge(rlo_ok, 1)
                pe.wait_ge(zlo_ok, T * grp + T)
                for h in range(HALVES):
                    cols = slice(h * 512, (h + 1) * 512)
                    if h:
                        pe.wait_ge(lgs_ok, HALVES * grp + h)
                    for k in range(KD):
                        pe.matmul(psT[:], r_hi[:, k, :], zhi[:, k, cols], start=(k == 0), stop=False)
                        pe.matmul(psT[:], r_hi[:, k, :], zlo[:, k, cols], start=False, stop=False)
                        mm = pe.matmul(psT[:], r_lo[:, k, :], zhi[:, k, cols], start=False, stop=(k == KD - 1))
                    mm.then_inc(lgt_ok, 1)
                    pe.wait_ge(lgs_ok, HALVES * grp + h + 1)
                    if h:
                        pe.wait_ge(lg_ok, HALVES * grp + h)
                    for t in range(TH):
                        mm = pe.transpose(psC[:, t * P:(t + 1) * P], lgT[:, t * P:(t + 1) * P], ident[:])
                    mm.then_inc(lgb_ok, 1)
                pe.wait_ge(cw_ok, grp + 1)
                for h in range(HALVES):
                    for t in range(TH):
                        mm = pe.transpose(psP[h][:, t * P:(t + 1) * P], cw[:, TH * h + t, :], ident[:])
                    mm.then_inc(cwt_ok, 1)
                pe.wait_ge(cwlo_ok, HALVES * (grp + 1))

            def product(out, w_hi, w_lo, k, cols, x_hi, x_lo, first, last):
                pe.matmul(out, w_hi(k), x_hi(k), start=first, stop=False)
                pe.matmul(out, w_hi(k), x_lo(k), start=False, stop=False)
                return pe.matmul(out, w_lo(k), x_hi(k), start=False, stop=last)

            def hidden(n, ahead):
                pe.wait_ge(guhi_ok, KD * (n + 1))
                pe.wait_ge(gulo_ok, KD * (n + 1))
                if GATE:
                    pe.wait_ge(spread_ok, n + 1)
                for i in range(CH):
                    j = CH * n + i
                    h, c = divmod(i, FC)
                    cols = slice(h * 512, (h + 1) * 512)
                    if isinstance(n, int) and n % units == 0 and c == 0:
                        pe.wait_ge(zlo_ok, T * (n // units) + TH * (h + 1))
                    for out, off, free, done in ((psG[i % 2], 0, silu_ok, gate_ok), (psU[i % 2], F, hid_ok, up_ok)):
                        w = slice(off + c * P, off + (c + 1) * P)
                        at_least(pe, free, j - 1 if i else j)
                        for k in range(KD):
                            mm = product(out[:], lambda k: gu_hi[:, k, w], lambda k: gu_lo[:, k, w], k, cols,
                                         lambda k: zhi[:, k, cols], lambda k: zlo[:, k, cols], k == 0, k == KD - 1)
                        mm.then_inc(done, 1)
                    if GATE:
                        at_least(pe, hid2_ok, j)
                        pe.matmul(psC[:], spread_r[:, c * P:(c + 1) * P], cwT[:, cols], start=True,
                                  stop=True).then_inc(cwb_ok, 1)

            def boundary(n, grp, current):
                prepared = grp is not None and grp < GROUPS
                before = n - 1
                for t in range(T):
                    if prepared:
                        tile(grp, t)
                    if grp == 0:
                        continue
                    if t == 0:
                        pe.wait_ge(dnhi_ok, n)
                        pe.wait_ge(dnlo_ok, n)
                    if t % TH == 0:
                        pe.wait_ge(hlo_ok, CH * before + FC * (t // TH + 1))
                    at_least(pe, acc_ok, T * before + (t - 1 if t else 0))
                    rows = slice(t * P, (t + 1) * P)
                    for c in range(FC):
                        mm = product(psD[t % 2][:], lambda c: h_hi[:, c, rows], lambda c: h_lo[:, c, rows], c, None,
                                     lambda c: dn_hi[:, c, :], lambda c: dn_lo[:, c, :], c == 0, c == FC - 1)
                    mm.then_inc(down_ok, 1)
                if GATE and prepared:
                    route(grp)

            each_group(pe, hidden, boundary)

        @block.vector
        def _(dve):
            dve.wait_ge(tanh_ok, 1)
            if GATE:
                dve.wait_ge(lower_ok, 1)
                dve.wait_ge(rhi_ok, 1)
                dve.tensor_tensor(r_lo[:], r_raw[:], r_hi[:], ALU.subtract).then_inc(rlo_ok, 1)

            def statistics(grp):
                dve.wait_ge(x_in[grp % 2], 16 * (grp // 2 + 1))
                at_least(dve, mv_ok, T * grp)
                for t in range(T):
                    dve.bn_stats(stats[:, t, :], xg[:, grp % 2, t, :]).then_inc(bn_ok, 1)
                at_least(dve, xn_ok, T * grp)
                for t in range(T):
                    dve.wait_ge(bn_ok, T * grp + t + 1)
                    dve.bn_aggr(mv[:, t, :], stats[:, t, :]).then_inc(mv_ok, 1)
                dve.wait_ge(mv_ok, T * grp + T)
                at_least(dve, rstd_ok, grp)
                dve.tensor_scalar(vare[:], mv[:, :, 1], EPS, None, ALU.add).then_inc(vare_ok, 1)

            def normalise(grp, t):
                if t == 0:
                    dve.wait_ge(rstd_ok, grp + 1)
                at_least(dve, zt_ok, T * grp + t - 1 if t else T * grp)
                dve.tensor_scalar(xn[:, t % 2, :], xg[:, grp % 2, t, :], mv[:, t, 0:1], rstd[:, t:t + 1],
                                  ALU.subtract, ALU.mult).then_inc(xn_ok, 1)

            def route(grp):
                for h in range(HALVES):
                    dve.wait_ge(lgb_ok, HALVES * grp + h + 1)
                    at_least(dve, exp_ok, grp)
                    dve.tensor_copy(lg[:, TH * h:TH * (h + 1), :],
                                    psC[:].rearrange("p (t w) -> p t w", t=TH)[:, :, 0:experts]).then_inc(lg_ok, 1)
                wide = lambda a: a[:].unsqueeze(2).broadcast_to((P, T, experts))
                dve.wait_ge(lg_ok, HALVES * (grp + 1))
                dve.tensor_reduce(mx[:], lg[:], AX.X, ALU.max).then_inc(sm_ok, 1)
                dve.wait_ge(sm_ok, 4 * grp + 1)
                dve.tensor_tensor(lg[:], lg[:], wide(mx), ALU.subtract).then_inc(sm_ok, 1)
                dve.wait_ge(exp_ok, grp + 1)
                dve.tensor_reduce(den[:], ex[:], AX.X, ALU.add).then_inc(sm_ok, 1)
                dve.wait_ge(sm_ok, 4 * grp + 3)
                dve.reciprocal(rden[:], den[:]).then_inc(sm_ok, 1)
                E = experts
                mine = ex[:].unsqueeze(3).broadcast_to((P, T, E, E))
                theirs = ex[:].unsqueeze(2).broadcast_to((P, T, E, E))
                at_least(dve, rank_ok, 6 * grp)
                dve.tensor_tensor(above[:], theirs, mine, ALU.is_gt).then_inc(rank_ok, 1)
                dve.tensor_tensor(same[:], theirs, mine, ALU.is_equal).then_inc(rank_ok, 1)
                dve.wait_ge(rank_ok, 6 * grp + 2)
                dve.tensor_tensor(same[:], same[:], lower[:].unsqueeze(1).broadcast_to((P, T, E, E)),
                                  ALU.mult).then_inc(rank_ok, 1)
                dve.wait_ge(rank_ok, 6 * grp + 3)
                dve.tensor_tensor(above[:], above[:], same[:], ALU.add).then_inc(rank_ok, 1)
                dve.wait_ge(rank_ok, 6 * grp + 4)
                dve.tensor_reduce(rank[:], above[:], AX.X, ALU.add).then_inc(rank_ok, 1)
                dve.wait_ge(rank_ok, 6 * grp + 5)
                at_least(dve, cw_ok, grp)
                dve.scalar_tensor_tensor(out=pick[:], in0=rank[:], scalar=float(TOP_K), in1=ex[:],
                                         op0=ALU.is_lt, op1=ALU.mult).then_inc(rank_ok, 1)
                dve.wait_ge(rank_ok, 6 * (grp + 1))
                dve.wait_ge(sm_ok, 4 * (grp + 1))
                at_least(dve, cwt_ok, HALVES * grp)
                dve.tensor_tensor(cw[:, :, 0:experts], pick[:], wide(rden), ALU.mult).then_inc(cw_ok, 1)
                for h in range(HALVES):
                    cols = slice(h * 512, (h + 1) * 512)
                    dve.wait_ge(cwhi_ok, HALVES * grp + h + 1)
                    dve.tensor_tensor(cwT[32:64, cols], psP[h][0:32, :], cwT[0:32, cols], ALU.subtract).then_inc(cwlo_ok, 1)

            def hidden(n, ahead):
                for i in range(CH + 1):
                    j = CH * n + i
                    u = i % 2
                    if i == CH // 2 and ahead is not None and ahead < GROUPS:
                        statistics(ahead)
                    if i < CH:
                        dve.wait_ge(silu_ok, j + 1)
                        dve.wait_ge(up_ok, j + 1)
                        if GATE:
                            dve.wait_ge(hid2_ok, j - 1 if i else j)
                        else:
                            dve.wait_ge(hhi_ok, j - 1 if i else j)
                            dve.wait_ge(hlo_ok, j - 1 if i else j)
                        dve.tensor_tensor(hid[:, u, :], psU[u][:], act_g[:, u, :], ALU.mult).then_inc(hid_ok, 1)
                        if GATE:
                            dve.wait_ge(hid_ok, j + 1)
                            dve.wait_ge(cwb_ok, j + 1)
                            dve.wait_ge(hhi_ok, j - 1 if i else j)
                            dve.wait_ge(hlo_ok, j - 1 if i else j)
                            dve.tensor_tensor(hid2[:, u, :], psC[:], hid[:, u, :], ALU.mult).then_inc(hid2_ok, 1)
                    if i > 0:
                        h, c = divmod(i - 1, FC)
                        cols = slice(h * 512, (h + 1) * 512)
                        dve.wait_ge(hhi_ok, j)
                        dve.tensor_tensor(h_lo[:, c, cols], src_h[:, (i - 1) % 2, :], h_hi[:, c, cols],
                                          ALU.subtract).then_inc(hlo_ok, 1)

            def boundary(n, grp, current):
                prepared = grp is not None and grp < GROUPS
                if prepared:
                    normalise(grp, 0)
                for t in range(T):
                    if prepared:
                        if t + 1 < T:
                            normalise(grp, t + 1)
                        rows = slice(t * P, (t + 1) * P)
                        dve.wait_ge(zhi_ok, T * grp + t + 1)
                        dve.tensor_tensor(zlo[:, :, rows], psP[t % 2][:].rearrange("p (k w) -> p k w", k=KD),
                                          zhi[:, :, rows], ALU.subtract).then_inc(zlo_ok, 1)
                    if grp != 0:
                        x = xg[:, current % 2, t, :]
                        dve.wait_ge(down_ok, T * (n - 1) + t + 1)
                        at_least(dve, acc_ok, T * (n - 1))
                        dve.scalar_tensor_tensor(out=x, in0=psD[t % 2][:], scalar=th[:, 0:1], in1=x,
                                                 op0=ALU.mult, op1=ALU.add).then_inc(acc_ok, 1)
                    if t % 2 == 0 and grp != GROUPS:
                        k = t // 2
                        dve.wait_ge(guhi_ok, KD * n + k + 1)
                        dve.tensor_tensor(gu_lo[:, k, :], gu_raw[:, k, :], gu_hi[:, k, :], ALU.subtract).then_inc(gulo_ok, 1)
                if grp == GROUPS:
                    return
                if GATE and prepared:
                    route(grp)
                dve.wait_ge(dnhi_ok, n + 1)
                dve.tensor_tensor(dn_lo[:], dn_raw[:], dn_hi[:], ALU.subtract).then_inc(dnlo_ok, 1)

            statistics(0)
            each_group(dve, hidden, boundary)




def rolled_from(eng, step, count, unroll, peel, lag):
    for t in range(peel * unroll):
        step(At(0, t, unroll, count))
    with eng.Fori(peel, count // unroll, 1) as k:
        for u in range(unroll):
            step(At(k, u, unroll, count))
    for u in range(lag):
        step(At(count // unroll, u, unroll, count))


def attention_phase(nc, x2, ctx_rows, mask, mask_t, w_qkv, b_qk, b_v, g, x3):
    HEADS, HD, GH = 16, 16, 4
    GROUPS = HEADS // GH
    N = B * GROUPS
    KC, TB = C // P, L // P
    NEG = 1.0e6
    HI, LO, HI2, MASK, MAX = 0, HD, 2 * HD, 3 * HD, 3 * HD + 3
    ROWS = 3 * HD + 4
    SPILLS = 12
    FOLD = 16
    PIECES = 6
    with ExitStack() as ctx:
        sb = lambda n, s, d=F32: ctx.enter_context(nc.sbuf_tensor(f"att_{n}", s, d))
        sem = ctx.enter_context(semaphores(nc, "att"))
        ps = lambda n, s: ctx.enter_context(nc.psum_tensor(f"att_{n}", s, F32))
        w_hi = sb("w_hi", [P, 3, KC, C], F32R); w_lo = sb("w_lo", [P, 3, KC, C], F32R)
        bqk = sb("bqk", [P, 4]); bqk4 = sb("bqk4", [P, 4]); bv = sb("bv", [P, C])
        gt = sb("gt", [P, 1]); th = sb("th", [P, 1]); ident = sb("ident", [P, P]); mhalf = sb("mhalf", [P, KC])
        xr = sb("xr", [P, KC, L]); cr = sb("cr", [P, KC, L])
        mbc = sb("mbc", [P, L]); mcol = sb("mcol", [P, TB])
        stats = sb("stats", [P, KC, 6]); mv = sb("mv", [P, KC, 2]); vare = sb("vare", [P, KC]); rstd = sb("rstd", [P, KC])
        xn = sb("xn", [P, KC, L])
        xn_hi = sb("xn_hi", [P, KC, L], F32R); xn_lo = sb("xn_lo", [P, KC, L], F32R)
        cr_hi = sb("cr_hi", [P, KC, L], F32R); cr_lo = sb("cr_lo", [P, KC, L], F32R)
        proj = sb("proj", [P, 4, L]); projm = sb("projm", [P, 2, L])
        p_hi = sb("p_hi", [P, 4, L], F32R); p_lo = sb("p_lo", [P, 4, L], F32R)
        mk = sb("mk", [B, L]); neg = sb("neg", [B, L])
        mcg = sb("mcg", [P, TB])
        qk = sb("qk", [P, 4, 2, GH, L], F32R)
        qs, ks = qk[:, :, 0], qk[:, :, 1]
        vtmp = sb("vtmp", [P, 2, 2, C]); va = sb("va", [P, 2, TB, HEADS, 2 * HD])
        nmax = sb("nmax", [P, 2, TB, GH]); mrow = sb("mrow", [GH, 2, L], F32R)
        pt = sb("pt", [P, 4, 2, L])
        osb = sb("osb", [P, 2, L]); rec = sb("rec", [P, L])
        den = sb("den", [P, FOLD]); rden = sb("rden", [P, FOLD]); mfold = sb("mfold", [P, FOLD]); rm = sb("rm", [P, FOLD])
        rec_rows = nc.dram_tensor("att_rec_rows", (GH, L), F32, kind="Internal").ap()
        lay = nc.dram_tensor("att_lay", (B, 2, ROWS, HEADS, L), F32, kind="Internal").ap()
        xs = sb("xs", [P, 2, L]); yo = sb("yo", [P, 2, L])
        psS = [ps(f"psS{i}", [P, L]) for i in range(3)]
        psB = [ps(f"psB{i}", [P, L]) for i in range(3)]
        bank = (0, 1, 2) * 5 + (1,)
        last_use = (4, 2, 4) + (3,) * 12 + (2,)
        psO = ps("psO", [P, L]); psM = ps("psM", [P, L])

        c_in = sem("c_in"); ident_zero = sem("ident_zero"); ident_ok = sem("ident_ok"); mhalf_ok = sem("mhalf_ok")
        zero_ok = sem("zero_ok"); tanh_ok = sem("tanh_ok"); whi_ok = sem("whi_ok"); wlo_ok = sem("wlo_ok"); bq_ok = sem("bq_ok")
        x_in = sem("x_in"); ctx_in = sem("ctx_in"); mask_in = sem("mask_in"); mcol_in = sem("mcol_in")
        bn_ok = sem("bn_ok"); mv_ok = sem("mv_ok"); vare_ok = sem("vare_ok"); rstd_ok = sem("rstd_ok"); xn_ok = sem("xn_ok")
        xhi_ok = sem("xhi_ok"); xlo_ok = sem("xlo_ok"); chi_ok = sem("chi_ok"); clo_ok = sem("clo_ok")
        mrow_ok = sem("mrow_ok"); mrow_out = sem("mrow_out"); lay_ok = sem("lay_ok"); mcg_ok = sem("mcg_ok")
        piece_ok = sem("piece_ok"); proj_ok = sem("proj_ok"); vtmp_ok = sem("vtmp_ok"); v_ok = sem("v_ok")
        projm_ok = sem("projm_ok"); phi_ok = sem("phi_ok"); plo_ok = sem("plo_ok")
        fill_in = [sem(f"fill_in{i}") for i in range(4)]
        s_ok = sem("s_ok"); max_ok = sem("max_ok"); mt_ok = sem("mt_ok"); mcopy_ok = sem("mcopy_ok")
        max_in = [sem(f"max_in{i}") for i in range(2)]
        b_ok = sem("b_ok"); exp_ok = sem("exp_ok"); av_ok = sem("av_ok")
        osb_ok = sem("osb_ok"); den_in = sem("den_in"); rden_ok = sem("rden_ok"); rm_ok = sem("rm_ok"); rm_out = sem("rm_out"); mk_in = sem("mk_in")
        rec_in = sem("rec_in"); out_ok = sem("out_ok"); y_ok = sem("y_ok")
        xs_in = [sem(f"xs_in{i}") for i in range(2)]
        stored = [sem(f"stored{i}") for i in range(2)]
        block = ctx.enter_context(nc.Block())
        roll = lambda eng, step: rolled_from(eng, step, N, 2 * GROUPS, 2, 9)
        raw = pt[:, 0:3, :, 0:C]
        element = lambda t: At(t.k, t.u // GROUPS, 2, B)

        @block.sync
        def _(sp):
            sp.dma_start(raw, w_qkv).then_inc(c_in, 16)
            sp.dma_start(bqk[:], b_qk).then_inc(c_in, 16)
            sp.dma_start(bv[:], b_v.broadcast_to((P, C))).then_inc(c_in, 16)
            sp.dma_start(gt[:], g).then_inc(c_in, 16)
            sp.dma_start(mk[:], mask).then_inc(mk_in, 16)

            def mask_rows_out():
                sp.wait_ge(mrow_ok, 8)
                for o in range(2):
                    for r in range(4):
                        sp.dma_start(lay[:, o, MASK + r], (p_lo if o else p_hi)[0:B, r, :].bitcast(F32).unsqueeze(1)
                                     .broadcast_to((B, HEADS, L))).then_inc(mrow_out, 16)

            def load(b):
                b4, pos = fixed(sp, 4 * b.n), fixed(sp, b.n * L, 4)
                at_least(sp, xn_ok, b.n)
                sp.dma_start(xr[:], bass.AP(tensor=x2.tensor, offset=pos,
                                            ap=[[B * L, P], [P * B * L, KC], [1, L]])).then_inc(x_in, 16)
                at_least(sp, clo_ok, b.n)
                sp.dma_start(cr[:], ctx_rows[bass.ds(b.n, 1)].rearrange("o (k p) s -> (o p) k s", p=P)).then_inc(ctx_in, 16)
                at_least(sp, mcg_ok, b.n)
                at_least(sp, projm_ok, b4)
                at_least(sp, v_ok, b4)
                sp.dma_start(mbc[:], mask[bass.ds(b.n, 1), :].broadcast_to((P, L))).then_inc(mask_in, 16)
                sp.dma_start(mcol[:], mask_t[bass.ds(b.n, 1)].rearrange("o p s -> (o p) s")).then_inc(mcol_in, 16)

            def spill(b, o):
                at, split = fixed(sp, b.n * 2 * ROWS * HEADS * L, 4), fixed(sp, 4 * b.n + 2 * (o + 1))
                sp.wait_ge(plo_ok, split)
                for row in (HI, LO, HI2):
                    part = p_lo if row == (HI2 if o else LO) else p_hi
                    for j in range(2):
                        sp.dma_start(bass.AP(tensor=lay.tensor, offset=at + ((o * ROWS + row) * HEADS + j * HEADS // 2) * L,
                                             ap=[[HEADS * L, HD], [L, HEADS // 2], [1, L]]),
                                     part[:, 2 * o + j, :].bitcast(F32)).then_inc(lay_ok, 16)

            def fill(f):
                b, s, a = element(f), f.of(4), f.u % GROUPS
                at = fixed(sp, b.n * 2 * ROWS * HEADS * L, 4)
                used, out = fixed(sp, 16 * (f.n - 3)), fixed(sp, 16 * SPILLS * (b.n + 1))
                if f.first(1):
                    sp.wait_ge(mrow_out, 16 * 8)
                    sp.wait_ge(zero_ok, 3)
                at_least(sp, b_ok, used)
                sp.wait_ge(lay_ok, out)
                for row, end in ((HI, MASK), (MASK, ROWS)):
                    sp.dma_start(qk[row:end, s].rearrange("p o h s -> p o (h s)").bitcast(F32),
                                 bass.AP(tensor=lay.tensor, offset=at + (row * HEADS + a * GH) * L,
                                         ap=[[HEADS * L, end - row], [ROWS * HEADS * L, 2], [1, GH * L]])).then_inc(fill_in[s], 16)

            def rows(w):
                b, s, a = element(w), w.of(2), w.u % GROUPS
                pos, before = fixed(sp, b.n * L, 4), fixed(sp, w.n - 1)
                if w.first(1):
                    sp.wait_ge(zero_ok, 3)
                at_least(sp, y_ok, before)
                for h in range(GH):
                    sp.dma_start(xs[32 * h:32 * h + HD, s, :],
                                 bass.AP(tensor=x2.tensor, offset=pos + (a * GH + h) * HD * B * L,
                                         ap=[[B * L, HD], [1, L]])).then_inc(xs_in[s], 16)

            def fold(w):
                pos, now, used = fixed(sp, element(w).n * L, 4), fixed(sp, w.n + 1), fixed(sp, w.n)
                sp.wait_ge(osb_ok, now)
                at_least(sp, rm_ok, used)
                sp.dma_start(den[:], osb[HD:P:32, w.of(2), :]).then_inc(den_in, 16)
                sp.dma_start(mfold[:], bass.AP(tensor=mask.tensor, offset=pos,
                                               ap=[[0, GH], [FOLD, L // FOLD], [1, FOLD]])).then_inc(den_in, 16)

            def unfold_out(w):
                now, used = fixed(sp, w.n + 1), fixed(sp, 16 * w.n)
                sp.wait_ge(rm_ok, now)
                at_least(sp, rec_in, used)
                sp.dma_start(rec_rows.rearrange("h (q c) -> (h q) c", c=FOLD), rm[:]).then_inc(rm_out, 16)

            def unfold_in(w):
                now, used = fixed(sp, 16 * (w.n + 1)), fixed(sp, w.n)
                sp.wait_ge(rm_out, now)
                at_least(sp, out_ok, used)
                sp.dma_start(rec[:], bass.AP(tensor=rec_rows.tensor, offset=0,
                                             ap=[[L, GH], [0, 32], [1, L]])).then_inc(rec_in, 16)

            def store(w):
                b, a = element(w), w.u % GROUPS
                pos = fixed(sp, b.n * L, 4)
                sp.wait_ge(y_ok, w.n + 1)
                for h in range(GH):
                    sp.dma_start(bass.AP(tensor=x3.tensor, offset=pos + (a * GH + h) * (HD // 4) * B * L,
                                         ap=[[B * L, HD // 4], [C // 4 * B * L, 4], [1, L]]),
                                 yo[32 * h:32 * h + HD, w.of(2), :]).then_inc(stored[w.of(2)], 16)

            def step(t):
                if t.back(4).there:
                    fill(t.back(4))
                if t.back(8).there:
                    fold(t.back(8))
                if t.u % GROUPS == 0 and t.there:
                    load(element(t))
                if t.first(1):
                    mask_rows_out()
                if t.u % GROUPS == 3 and t.there:
                    spill(element(t), 0)
                if t.back(8).there:
                    rows(t.back(8))
                if t.back(9).there:
                    store(t.back(9))
                if t.back(8).there:
                    unfold_out(t.back(8))
                if t.u % GROUPS == 3 and t.there:
                    spill(element(t), 1)
                if t.back(8).there:
                    unfold_in(t.back(8))

            roll(sp, step)
            for i in range(2):
                sp.wait_ge(stored[i], 16 * GH * (N // 2))

        @block.gpsimd
        def _(pool):
            pool.memset(ident[:], 0.0).then_inc(ident_zero, 1)
            pool.memset(mhalf[:], -0.5).then_inc(mhalf_ok, 1)
            pool.wait_ge(ident_zero, 1)
            pool.affine_select(out=ident[:], in_=ident[:], compare_op=ALU.not_equal, fill=1.0, base=0,
                               pattern=[[-1, P]], channel_multiplier=1).then_inc(ident_ok, 1)
            pool.wait_ge(c_in, 64)
            pool.wait_ge(whi_ok, 1)
            pool.tensor_tensor(w_lo[:], raw, w_hi[:], ALU.subtract).then_inc(wlo_ok, 1)
            pool.wait_ge(mhalf_ok, 1)
            pool.memset(qk[:].bitcast(F32), 0.0).then_inc(zero_ok, 1)
            pool.memset(xs[:], 0.0).then_inc(zero_ok, 1)

            def finish(w):
                s = w.of(2)
                pool.wait_ge(osb_ok, w.n + 1)
                pool.wait_ge(rec_in, 16 * (w.n + 1))
                pool.tensor_tensor(osb[:, s, :], osb[:, s, :], rec[:], ALU.mult).then_inc(out_ok, 1)
                pool.wait_ge(out_ok, w.n + 1)
                pool.wait_ge(xs_in[s], 16 * GH * (w.use(2) + 1))
                at_least(pool, stored[s], 16 * GH * w.use(2))
                pool.tensor_tensor(yo[:, s, :], osb[:, s, :], xs[:, s, :], ALU.add).then_inc(y_ok, 1)

            def step(t):
                a, b = t.u % GROUPS, element(t)
                if t.back(9).there:
                    finish(t.back(9))
                if not t.there:
                    return
                if a == 0:
                    pool.wait_ge(vare_ok, b.n + 1)
                    at_least(pool, xn_ok, b.n)
                    pool.tensor_tensor(rstd[:], vare[:], mhalf[:], ALU.pow).then_inc(rstd_ok, 1)
                if a == 1:
                    pool.wait_ge(xhi_ok, b.n + 1)
                    at_least(pool, piece_ok, PIECES * b.n)
                    pool.tensor_tensor(xn_lo[:], xn[:], xn_hi[:], ALU.subtract).then_inc(xlo_ok, 1)
                    pool.wait_ge(chi_ok, b.n + 1)
                    pool.tensor_tensor(cr_lo[:], cr[:], cr_hi[:], ALU.subtract).then_inc(clo_ok, 1)
                if a == 2:
                    for p in range(5):
                        if p < 4:
                            pool.wait_ge(proj_ok, 4 * b.n + p + 1)
                            pool.wait_ge(mask_in, 16 * (b.n + 1))
                            at_least(pool, plo_ok, 4 * b.n + p - 1)
                            pool.tensor_tensor(projm[:, p % 2, :], proj[:, p, :], mbc[:], ALU.mult).then_inc(projm_ok, 1)
                        if p > 0:
                            pool.wait_ge(phi_ok, 4 * b.n + p)
                            if p == 1 and b.first(1):
                                pool.wait_ge(mrow_out, 16 * 8)
                            if p == 1:
                                at_least(pool, lay_ok, 16 * SPILLS * b.n)
                            pool.tensor_tensor(p_lo[:, p - 1, :], projm[:, (p - 1) % 2, :], p_hi[:, p - 1, :],
                                               ALU.subtract).then_inc(plo_ok, 1)

            roll(pool, step)

        @block.scalar
        def _(act):
            act.wait_ge(c_in, 64)
            act.activation(th[:], gt[:], ACT.Tanh).then_inc(tanh_ok, 1)
            act.activation(w_hi[:], raw, ACT.Copy).then_inc(whi_ok, 1)
            act.wait_ge(wlo_ok, 1)
            act.wait_ge(bq_ok, 1)

            def step(t):
                a, b = t.u % GROUPS, element(t)
                m, e, w = t.back(6), t.back(7), t.back(8)
                for j in range(8):
                    if j == 1 and w.there:
                        act.wait_ge(av_ok, TB * (w.n + 1))
                        at_least(act, y_ok, w.n - 1)
                        act.activation(osb[:, w.of(2), :], psO[:], ACT.Copy).then_inc(osb_ok, 1)
                    if e.there:
                        at_least(act, av_ok, 4 * e.n + j // 2 - 1)
                        for i in (2 * j, 2 * j + 1):
                            act.wait_ge(b_ok, 16 * e.n + i + 1)
                            act.activation(pt[:, j % 4, i % 2, :], psB[bank[i]][:], ACT.Exp).then_inc(exp_ok, 1)
                    if j == 0 and m.there:
                        act.wait_ge(mt_ok, m.n + 1)
                        at_least(act, max_in[m.of(2)], 16 * m.use(2))
                        act.activation(mrow[:, m.of(2), :], psM[0:GH, :], ACT.Copy).then_inc(mcopy_ok, 1)
                        act.wait_ge(mcopy_ok, m.n + 1)
                        act.dma_start(qs[MAX:MAX + 1, m.of(4), :, :].bitcast(F32),
                                      mrow[:, m.of(2), :].bitcast(F32)).then_inc(max_in[m.of(2)], 16)
                    if a == 2 and t.there and 2 <= j < 6:
                        p = j - 2
                        act.wait_ge(piece_ok, PIECES * b.n + p + 1)
                        at_least(act, projm_ok, 4 * b.n)
                        scale = 1.0 / HD ** 0.5 if p < 2 else 1.0
                        bias = bqk4 if p < 2 else bqk
                        act.activation(proj[:, p, :], psM[:], ACT.Identity, bias=bias[:, p:p + 1],
                                       scale=scale).then_inc(proj_ok, 1)
                    if a == 3 and t.there and j >= 4:
                        s = j - 4
                        act.wait_ge(vtmp_ok, 2 * b.n + s // 2 + 1)
                        act.wait_ge(mcg_ok, b.n + 1)
                        at_least(act, av_ok, 16 * (b.n - 1))
                        act.activation(va[:, b.of(2), s, :, 0:HD], vtmp[:, s // 2, s % 2, :].rearrange("p (h d) -> p h d", h=HEADS),
                                       ACT.Copy, scale=mcg[:, s:s + 1]).then_inc(v_ok, 1)

            roll(act, step)

        @block.tensor
        def _(pe):
            pe.wait_ge(ident_ok, 1)
            pe.wait_ge(wlo_ok, 1)
            pe.wait_ge(zero_ok, 3)

            def project(b, p):
                at_least(pe, mcopy_ok, 4 * b.n + p // 4 - 3)
                if p == 0:
                    pe.wait_ge(xlo_ok, b.n + 1)
                    pe.wait_ge(clo_ok, b.n + 1)
                if 1 <= p < 5:
                    pe.wait_ge(proj_ok, 4 * b.n + p)
                if p == 5:
                    pe.wait_ge(vtmp_ok, 2 * b.n + 1)
                if p < 4:
                    w, o = divmod(p, 2)
                    hi, lo = (xn_hi, xn_lo) if w == 0 else (cr_hi, cr_lo)
                    cols = slice(o * P, (o + 1) * P)
                    for k in range(KC):
                        for x, y in ((w_hi, hi), (w_hi, lo), (w_lo, hi)):
                            mm = pe.matmul(psM[:], x[:, w, k, cols], y[:, k, :], start=(k == 0 and x is w_hi and y is hi),
                                           stop=(k == KC - 1 and x is w_lo))
                else:
                    for s in range(2):
                        rows = slice(((p - 4) * 2 + s) * P, ((p - 4) * 2 + s + 1) * P)
                        for k in range(KC):
                            for x, y in ((cr_hi, w_hi), (cr_lo, w_hi), (cr_hi, w_lo)):
                                mm = pe.matmul(psM[:, s * C:(s + 1) * C], x[:, k, rows], y[:, 2, k, :],
                                               start=(k == 0 and x is cr_hi and y is w_hi), stop=(k == KC - 1 and y is w_lo))
                mm.then_inc(piece_ok, 1)

            def outputs(n, s):
                b, a = element(n), n.u % GROUPS
                pe.wait_ge(exp_ok, 16 * n.n + GH * (s + 1))
                if s == 0:
                    pe.wait_ge(v_ok, TB * (b.n + 1))
                    at_least(pe, osb_ok, n.n)
                for h in range(GH):
                    mm = pe.matmul(psO[32 * h:32 * h + 32, :], va[:, b.of(2), s, a * GH + h, :],
                                   pt[:, (2 * s + h // 2) % 4, h % 2, :], start=(s == 0), stop=(s == TB - 1))
                mm.then_inc(av_ok, 1)

            def step(t):
                a, b = t.u % GROUPS, element(t)
                s, m, e, w = t.back(5), t.back(6), t.back(7), t.back(8)
                for i in range(16):
                    if i == 1 and m.there:
                        pe.wait_ge(max_ok, 16 * (m.n + 1))
                        at_least(pe, mcopy_ok, m.n)
                        if a == 3 and t.there:
                            pe.wait_ge(proj_ok, 4 * (b.n + 1))
                        if a == 0 and t.back(1).there:
                            at_least(pe, vtmp_ok, 2 * b.n)
                        for k in range(TB):
                            mm = pe.transpose(psM[0:GH, k * P:(k + 1) * P], nmax[:, m.of(2), k, :], ident[:])
                        mm.then_inc(mt_ok, 1)
                    if s.there:
                        if i == 0:
                            pe.wait_ge(fill_in[s.of(4)], 32 * (s.use(4) + 1))
                        h, k = divmod(i, TB)
                        at_least(pe, max_ok, 16 * s.n + i + 1 - last_use[i])
                        pe.matmul(psS[bank[i]][:], qs[:, s.of(4), h, k * P:(k + 1) * P], ks[:, s.of(4), h, :],
                                  start=True, stop=True).then_inc(s_ok, 1)
                    if e.there:
                        if i == 0:
                            pe.wait_ge(max_in[e.of(2)], 16 * (e.use(2) + 1))
                        k, h = divmod(i, GH)
                        at_least(pe, exp_ok, 16 * e.n + i + 1 - last_use[i])
                        pe.matmul(psB[bank[i]][:], ks[:, e.of(4), h, k * P:(k + 1) * P],
                                       qs[:, e.of(4), h, :], start=True, stop=True).then_inc(b_ok, 1)
                    if i in (0, 3) and w.there:
                        outputs(w, 2 if i == 0 else 3)
                    if i in (8, 12) and e.there:
                        outputs(e, (i - 8) // 4)
                    if a == 2 and t.there and i in (3, 6, 9, 12):
                        project(b, (i - 3) // 3)
                    if a == 3 and t.there and i in (4, 9):
                        project(b, 4 + (i - 4) // 5)

            roll(pe, step)

        @block.vector
        def _(dve):
            dve.wait_ge(c_in, 64)
            dve.tensor_scalar(bqk4[:], bqk[:], 1.0 / HD ** 0.5, None, ALU.mult).then_inc(bq_ok, 1)
            dve.memset(va[:], 1.0).then_inc(zero_ok, 1)
            dve.wait_ge(mk_in, 16)
            q_rows, k_rows = p_hi[0:B], p_lo[0:B]
            dve.tensor_scalar(neg[:], mk[:], -1.0, NEG, ALU.add, ALU.mult).then_inc(mrow_ok, 1)
            dve.tensor_copy(q_rows[:, 0, :], mk[:]).then_inc(mrow_ok, 1)
            dve.tensor_copy(q_rows[:, 1, :], mk[:])
            dve.memset(q_rows[:, 3, :].bitcast(F32), 0.0).then_inc(mrow_ok, 1)
            dve.memset(k_rows[:, 3, :].bitcast(F32), 1.0).then_inc(mrow_ok, 1)
            dve.wait_ge(mrow_ok, 4)
            dve.tensor_tensor(q_rows[:, 2, :], mk[:], q_rows[:, 0, :], ALU.subtract).then_inc(mrow_ok, 1)
            dve.tensor_copy(k_rows[:, 0, :], neg[:]).then_inc(mrow_ok, 1)
            dve.tensor_copy(k_rows[:, 2, :], neg[:]).then_inc(mrow_ok, 1)
            dve.wait_ge(mrow_ok, 7)
            dve.tensor_tensor(k_rows[:, 1, :], neg[:], k_rows[:, 0, :], ALU.subtract).then_inc(mrow_ok, 1)
            dve.wait_ge(tanh_ok, 1)

            def step(t):
                a, b = t.u % GROUPS, element(t)
                s, w = t.back(5), t.back(8)
                for i in range(16):
                    if s.there:
                        h, k = divmod(i, TB)
                        dve.wait_ge(s_ok, 16 * s.n + i + 1)
                        at_least(dve, mt_ok, s.n - 1)
                        dve.tensor_reduce(nmax[:, s.of(2), k, h:h + 1], psS[bank[i]][:], AX.X, ALU.max,
                                          negate=True).then_inc(max_ok, 1)
                    if i == 13 and w.there:
                        dve.wait_ge(den_in, 32 * (w.n + 1))
                        dve.reciprocal(rden[:], den[:]).then_inc(rden_ok, 1)
                        dve.wait_ge(rden_ok, w.n + 1)
                        at_least(dve, rm_out, 16 * w.n)
                        dve.tensor_tensor(rm[:], rden[:], mfold[:], ALU.mult).then_inc(rm_ok, 1)
                    if not t.there:
                        continue
                    if a == 0 and i == 13:
                        dve.wait_ge(x_in, 16 * (b.n + 1))
                        for c in range(KC):
                            at_least(dve, mv_ok, KC * b.n)
                            dve.bn_stats(stats[:, c, :], xr[:, c, :]).then_inc(bn_ok, 1)
                    if a == 0 and i == 15:
                        for c in range(KC):
                            now, before = fixed(dve, KC * (b.n + 1)), fixed(dve, b.n)
                            dve.wait_ge(tanh_ok, 1)
                            dve.wait_ge(bn_ok, now)
                            at_least(dve, xn_ok, before)
                            dve.bn_aggr(mv[:, c, :], stats[:, c, :]).then_inc(mv_ok, 1)
                        dve.wait_ge(mv_ok, KC * (b.n + 1))
                        at_least(dve, rstd_ok, b.n)
                        dve.tensor_scalar(vare[:], mv[:, :, 1], EPS, None, ALU.add).then_inc(vare_ok, 1)
                    if a == 1 and i == 2:
                        dve.wait_ge(rstd_ok, b.n + 1)
                        at_least(dve, xlo_ok, b.n)
                        for c in range(KC):
                            mm = dve.tensor_scalar(xn[:, c, :], xr[:, c, :], mv[:, c, 0:1], rstd[:, c:c + 1],
                                                   ALU.subtract, ALU.mult)
                        mm.then_inc(xn_ok, 1)
                    if a == 1 and i == 6:
                        dve.wait_ge(xn_ok, b.n + 1)
                        at_least(dve, piece_ok, PIECES * b.n)
                        dve.tensor_copy(xn_hi[:], xn[:]).then_inc(xhi_ok, 1)
                        dve.wait_ge(ctx_in, 16 * (b.n + 1))
                        dve.tensor_copy(cr_hi[:], cr[:]).then_inc(chi_ok, 1)
                    if a == 3 and i == 3:
                        dve.wait_ge(mcol_in, 16 * (b.n + 1))
                        at_least(dve, v_ok, TB * b.n)
                        dve.tensor_scalar(mcg[:], mcol[:], th[:, 0:1], None, ALU.mult).then_inc(mcg_ok, 1)
                    if a == 2 and i in (10, 14) or a == 3 and i in (2, 6):
                        p = (0 if a == 2 else 2) + (i in (14, 6))
                        dve.wait_ge(projm_ok, 4 * b.n + p + 1)
                        if p == 0 and b.first(1):
                            dve.wait_ge(mrow_out, 16 * 8)
                        if p == 0:
                            at_least(dve, lay_ok, 16 * SPILLS * b.n)
                        dve.tensor_copy(p_hi[:, p, :], projm[:, p % 2, :]).then_inc(phi_ok, 1)
                    if a == 3 and i in (6, 11):
                        r = (i - 6) // 5
                        dve.wait_ge(piece_ok, PIECES * b.n + 5 + r)
                        at_least(dve, v_ok, TB * b.n)
                        dve.tensor_tensor(vtmp[:, r], psM[:].rearrange("p (s c) -> p s c", s=2),
                                          bv[:].unsqueeze(1).broadcast_to((P, 2, C)), ALU.add).then_inc(vtmp_ok, 1)

            roll(dve, step)


def build(nc, x, ctx_t, ctx_rows, taps, skip, mask, mask_t, router, spread, moe_gu, moe_dn, w_qkv, b_qk, b_v,
          ffn_gu, ffn_dn, g, out):
    rows = [nc.dram_tensor(f"rows{i}", (C * B, L), F32, kind="Internal").ap() for i in range(3)]
    taps_pad = nc.dram_tensor("taps_pad", (32, L + P), F32, kind="Internal").ap()
    group = lambda a: lambda n: a[bass.ds(n * 1024, 1024), :].rearrange("(t p) d -> p t d", p=P)
    mix_phase(nc, x, ctx_t, taps, skip, g[0], taps_pad, rows[0])
    ffn_phase(nc, "moe", group(rows[0]), group(rows[1]), moe_gu, moe_dn, 5, 3, g[1], 8, router, spread)
    attention_phase(nc, rows[1], ctx_rows, mask, mask_t, w_qkv, b_qk, b_v, g[2], rows[2])
    ffn_phase(nc, "ffn", group(rows[2]), group(out), ffn_gu, ffn_dn, 1, 4, g[3])


def kernel(**inputs):
    import numpy as np
    import concourse.bacc as bacc
    from concourse.bass_utils import run_bass_kernel_spmd

    a = {k: np.asarray(v) for k, v in inputs.items()}
    x, c = a["x"], a["ctx_2048"]
    mask = a["mask_Bx1x2048_fk1"].reshape(B, L)
    pair = lambda w: w.reshape(4, 2, 512, 192).transpose(0, 2, 1, 3).reshape(4, 512, 384)
    gate = np.concatenate([pair(a["L0_ffn_w_gate"]), a["L0_ffn_shared_gate"][None]])
    up = np.concatenate([pair(a["L0_ffn_w_up"]), a["L0_ffn_shared_up"][None]])
    down = np.concatenate([a["L0_ffn_w_down"].reshape(4, 384, 512), a["L0_ffn_shared_down"][None]])
    spread = np.zeros((5, P, 384), np.float32)
    for u in range(5):
        for f in range(384):
            e = 8 if u == 4 else 2 * u + f // 192
            spread[u, e, f] = spread[u, 32 + e, f] = 1.0
    turn = lambda w: w.reshape(w.shape[:-1] + (2, 8, 16)).swapaxes(-1, -2).reshape(w.shape)
    wq, wk, wv = (f(a[f"L1_xattn_W{n}"].T).reshape(2, P, C) for n, f in (("q", turn), ("k", turn), ("v", lambda w: w)))
    bq, bk = (turn(a[f"L1_xattn_b{n}"]).reshape(2, P) for n in "qk")
    g = np.stack([a["g_xattn"][0], a["g_ffn"][0], a["g_xattn"][1], a["g_ffn"][1]])
    arrays = {
        "x": x.transpose(1, 0, 2).reshape(C * B, L),
        "ctx_t": c.reshape(B, 32, 8, 4, P)[..., ::-1].transpose(1, 4, 3, 2, 0).reshape(32, P, 4, P),
        "ctx_rows": c,
        "taps": a["L0_xattn_ssm_kernel"],
        "skip": a["L0_xattn_D"].reshape(32, 1),
        "mask": mask,
        "mask_t": mask.reshape(B, 4, P).transpose(0, 2, 1),
        "router": a["L0_ffn_router"].reshape(4, P, 8).transpose(1, 0, 2),
        "spread": spread,
        "moe_gu": np.concatenate([gate, up], 2).reshape(5, 4, P, 768).transpose(0, 2, 1, 3),
        "moe_dn": down.reshape(5, 3, P, 512).transpose(0, 2, 1, 3),
        "w_qkv": np.stack([wq, wk, wv]).transpose(2, 0, 1, 3),
        "b_qk": np.stack([bq[0], bq[1], bk[0], bk[1]], 1),
        "b_v": a["L1_xattn_bv"].reshape(1, C),
        "ffn_gu": a["L1_ffn_gate_up_proj"].reshape(4, 4, P, 1024).transpose(0, 2, 1, 3),
        "ffn_dn": a["L1_ffn_down_proj"].reshape(4, 4, P, 512).transpose(0, 2, 1, 3),
        "g": np.broadcast_to(g[:, None, None], (4, P, 1)),
    }
    arrays = {f"in_{k}": np.ascontiguousarray(v) for k, v in arrays.items()}
    nc = bacc.Bacc("TRN2", target_bir_lowering=False, num_devices=1)
    args = [nc.dram_tensor(k, v.shape, mybir.dt.from_np(v.dtype), kind="ExternalInput").ap() for k, v in arrays.items()]
    out = nc.dram_tensor("out_rows", (C * B, L), F32, kind="ExternalOutput").ap()
    build(nc, *args, out)
    r = run_bass_kernel_spmd(nc, [arrays], core_ids=[0])
    y = r.results[0]["out_rows"].reshape(4, C // 4, B, L)
    return np.ascontiguousarray(y.transpose(2, 1, 0, 3)).reshape(B, C, L)
```
